# Optimizing a Trainium2 kernel written in Bass

```python
import numpy as np
import jax
import jax.numpy as jnp

def _softmax(x, axis=-1):
    return jax.nn.softmax(x, axis=axis)

def _gelu(x):
    return jax.nn.gelu(x, approximate=True)

def _silu(x):
    return jax.nn.silu(x)

def _sigmoid(x):
    return jax.nn.sigmoid(x)

def _layernorm(x, axis=-1, eps=1e-05):
    m = jnp.mean(x, axis=axis, keepdims=True)
    v = jnp.var(x, axis=axis, keepdims=True)
    return (x - m) / jnp.sqrt(v + eps)

def _scatter_add(tgt, idx, src, axis=0):
    return tgt.at[idx].add(src)

def _segment_sum(src, seg, n):
    return jax.ops.segment_sum(src, seg, n)
kernel_name = 'mk_decoder_postln_d2_seqx_r8_f2d658'

def setup_inputs(seed: int=0):
    np.random.seed(seed)
    _w = jnp.asarray

    def _rec_inputs():
        import jax
        import jax.numpy as jnp
        _rk = jax.random.key(seed)
        x = -7.109e-05 + 0.9999 * jax.random.normal(jax.random.fold_in(_rk, 1), (4, 256, 256), jnp.float32)
        _lenS = 256 - jax.random.randint(jax.random.fold_in(_rk, 7), (4,), 0, max(1, 256 // 4) + 1, jnp.int32)
        _lenS2 = 256 - jax.random.randint(jax.random.fold_in(_rk, 8), (4,), 0, max(1, 256 // 4) + 1, jnp.int32)
        _ctx_512P = jax.random.normal(jax.random.fold_in(_rk, 11), (4, 16, 64), jnp.float32)
        _ctx_512c = jax.random.dirichlet(jax.random.fold_in(_rk, 511), 0.3 * jnp.ones((16,), jnp.float32), (4, 256))
        _ctx_512t = jnp.einsum('bsk,bkd->bsd', _ctx_512c, _ctx_512P)
        _ctx_512t = _ctx_512t * jax.lax.rsqrt(jnp.mean(jnp.square(_ctx_512t)) + 1e-12) * 0.953939
        ctx_512 = 2.81802e-05 + 1.00001 * (_ctx_512t + 0.3 * jax.random.normal(jax.random.fold_in(_rk, 611), (4, 256, 64), jnp.float32))
        return (x, ctx_512)
    x, ctx_512 = _rec_inputs()

    def _L0_attn_setup():
        import jax, jax.numpy as jnp
        import numpy as np
        BLOCK = 32
        EPS = 1e-06

        def _silu(x):
            return x * jax.nn.sigmoid(x)
        key = jax.random.key(seed)
        k1, k2, k3, k4 = jax.random.split(key, 4)
        embed_dim, hidden_dim = (256, 256)
        b, n, h = (2, 512, 16)
        x = jax.random.normal(k1, (b, n, embed_dim), dtype=jnp.float32)
        slope_rate = jax.random.uniform(k2, (h, 1, 1), dtype=jnp.float32, minval=0.01, maxval=1.0)
        W_qkvu = jax.random.normal(k3, (4 * hidden_dim, embed_dim), dtype=jnp.float32) / np.sqrt(embed_dim)
        W_out = jax.random.normal(k4, (embed_dim, hidden_dim), dtype=jnp.float32) / np.sqrt(hidden_dim)
        return {'x': x, 'slope_rate': slope_rate, 'W_qkvu': W_qkvu, 'W_out': W_out}
    _L0_attn_all = _L0_attn_setup()
    _L0_attn_in = {k: v for k, v in _L0_attn_all.items() if k in ('slope_rate', 'W_qkvu', 'W_out')}
    del _L0_attn_all

    def _L0_xattn_setup():
        import jax, jax.numpy as jnp
        import numpy as np
        EPS = 1e-06
        IMAGE_DIMS = 256
        key = jax.random.key(seed)
        k1, k2, k3 = jax.random.split(key, 3)
        B, I, J, D = (16, 256, 256, 64)
        p = jax.random.normal(k1, (B, I, J), dtype=jnp.float32)
        k_v = jax.random.normal(k2, (B, J, D), dtype=jnp.float32)
        W_k = jax.random.normal(k3, (D, D), dtype=jnp.float32) * (1.0 / np.sqrt(D))
        b_k = jnp.zeros((D,), dtype=jnp.float32)
        ln_gamma = jnp.ones((J,), dtype=jnp.float32)
        ln_beta = jnp.zeros((J,), dtype=jnp.float32)
        return {'p': p, 'k_v': k_v, 'W_k': W_k, 'b_k': b_k, 'ln_gamma': ln_gamma, 'ln_beta': ln_beta}
    _L0_xattn_all = _L0_xattn_setup()
    _L0_xattn_in = {k: v for k, v in _L0_xattn_all.items() if k in ('W_k', 'b_k', 'ln_gamma', 'ln_beta')}
    del _L0_xattn_all

    def _L0_ffn_setup():
        import jax, jax.numpy as jnp
        import numpy as np
        B, L, D = (2, 128, 256)
        E, TOP_K, RANK, DFF = (8, 2, 8, 688)

        def _lora(x, A, Bm, scale):
            return x @ A @ Bm * scale

        def _expert_lora(x, A, Bm, w, scale):
            xA = jnp.einsum('bld,edr->bler', x, A)
            xAB = jnp.einsum('bler,erd->bled', xA, Bm) * scale
            return (xAB * w).sum(axis=2)
        key = jax.random.key(seed)
        ks = jax.random.split(key, 18)
        r = lambda k, s, sc: jax.random.normal(k, s, dtype=jnp.float32) * sc
        inv_d = 1.0 / np.sqrt(D)
        inv_f = 1.0 / np.sqrt(DFF)
        return {'x': r(ks[0], (B, L, D), 1.0), 'W_router': r(ks[1], (D, E), inv_d), 'W_gate': r(ks[2], (D, DFF), inv_d), 'W_up': r(ks[3], (D, DFF), inv_d), 'W_down': r(ks[4], (DFF, D), inv_f), 'sA_gate': r(ks[5], (D, RANK), inv_d), 'sB_gate': r(ks[6], (RANK, DFF), 0.02), 'sA_up': r(ks[7], (D, RANK), inv_d), 'sB_up': r(ks[8], (RANK, DFF), 0.02), 'sA_down': r(ks[9], (DFF, RANK), inv_f), 'sB_down': r(ks[10], (RANK, D), 0.02), 'A_gate': r(ks[11], (E, D, RANK), inv_d), 'B_gate': r(ks[12], (E, RANK, DFF), 0.02), 'A_up': r(ks[13], (E, D, RANK), inv_d), 'B_up': r(ks[14], (E, RANK, DFF), 0.02), 'A_down': r(ks[15], (E, DFF, RANK), inv_f), 'B_down': r(ks[16], (E, RANK, D), 0.02), 'expert_bias': jnp.zeros((E,), dtype=jnp.float32)}
    _L0_ffn_all = _L0_ffn_setup()
    _L0_ffn_in = {k: v for k, v in _L0_ffn_all.items() if k in ('W_router', 'W_gate', 'W_up', 'W_down', 'sA_gate', 'sB_gate', 'sA_up', 'sB_up', 'sA_down', 'sB_down', 'A_gate', 'B_gate', 'A_up', 'B_up', 'A_down', 'B_down', 'expert_bias')}
    del _L0_ffn_all

    def _L1_attn_setup():
        import jax, jax.numpy as jnp
        import numpy as np
        D_MODEL = 256
        D_INNER = 512
        D_STATE = 16
        DT_RANK = 128
        D_CONV = 4
        EPS = 1e-05

        def _rmsnorm(x, w):
            return x * jax.lax.rsqrt(jnp.mean(jnp.square(x), axis=-1, keepdims=True) + EPS) * w

        def _depthwise_causal_conv(x, conv_w, conv_b):
            k = conv_w[:, None, :]
            y = jax.lax.conv_general_dilated(x, k, window_strides=(1,), padding=((D_CONV - 1, 0),), dimension_numbers=('NWC', 'WIO', 'NWC'), feature_group_count=D_INNER)
            return y + conv_b

        def _selective_scan(u, delta, A, B, C, D):
            deltaA = jnp.exp(jnp.einsum('bld,dn->bldn', delta, A))
            deltaBu = jnp.einsum('bld,bln,bld->bldn', delta, B, u)
            dA = jnp.moveaxis(deltaA, 1, 0)
            dBu = jnp.moveaxis(deltaBu, 1, 0)
            Ct = jnp.moveaxis(C, 1, 0)
            b, l, d = u.shape
            n = A.shape[1]

            def step(h, inputs):
                dA_t, dBu_t, C_t = inputs
                h = h * dA_t + dBu_t
                y = jnp.einsum('bdn,bn->bd', h, C_t)
                return (h, y)
            h0 = jnp.zeros((b, d, n), u.dtype)
            _, ys = jax.lax.scan(step, h0, (dA, dBu, Ct))
            y = jnp.moveaxis(ys, 0, 1)
            return y + u * D
        key = jax.random.key(seed)
        ks = jax.random.split(key, 10)
        b, l = (1, 128)
        s = 0.02
        x = jax.random.normal(ks[0], (b, l, D_MODEL), jnp.float32)
        w_norm = jnp.ones((D_MODEL,), jnp.float32)
        W_in = jax.random.normal(ks[1], (D_MODEL, 2 * D_INNER), jnp.float32) * s
        conv_w = jax.random.normal(ks[2], (D_CONV, D_INNER), jnp.float32) * 0.3
        conv_b = jnp.zeros((D_INNER,), jnp.float32)
        W_xp = jax.random.normal(ks[3], (D_INNER, DT_RANK + 2 * D_STATE), jnp.float32) * s
        W_dt = jax.random.normal(ks[4], (DT_RANK, D_INNER), jnp.float32) * s
        b_dt = jnp.full((D_INNER,), -4.0, jnp.float32)
        A_log = jnp.log(jnp.tile(jnp.arange(1, D_STATE + 1, dtype=jnp.float32), (D_INNER, 1)))
        D = jnp.ones((D_INNER,), jnp.float32)
        W_out = jax.random.normal(ks[5], (D_INNER, D_MODEL), jnp.float32) * s
        return dict(x=x, w_norm=w_norm, W_in=W_in, conv_w=conv_w, conv_b=conv_b, W_xp=W_xp, W_dt=W_dt, b_dt=b_dt, A_log=A_log, D=D, W_out=W_out)
    _L1_attn_all = _L1_attn_setup()
    _L1_attn_in = {k: v for k, v in _L1_attn_all.items() if k in ('w_norm', 'W_in', 'conv_w', 'conv_b', 'W_xp', 'W_dt', 'b_dt', 'A_log', 'D', 'W_out')}
    del _L1_attn_all

    def _L1_xattn_setup():
        import jax, jax.numpy as jnp
        import numpy as np
        import math
        NUM_Q_HEADS = 32
        NUM_KV_HEADS = 8
        key = jax.random.key(seed)
        k1, k2, k3 = jax.random.split(key, 3)
        B, S, E = (2, 256, 256)
        kv_E = NUM_KV_HEADS * (E // NUM_Q_HEADS)
        q = jax.random.normal(k1, (B, S, E), dtype=jnp.float32)
        k = jax.random.normal(k2, (B, S, kv_E), dtype=jnp.float32)
        v = jax.random.normal(k3, (B, S, kv_E), dtype=jnp.float32)
        return {'q': q, 'k': k, 'v': v}
    _L1_xattn_all = _L1_xattn_setup()
    _L1_xattn_in = {k: v for k, v in _L1_xattn_all.items() if k in ()}
    del _L1_xattn_all

    def _L1_ffn_setup():
        import jax, jax.numpy as jnp
        import numpy as np
        B, S, H = (2, 256, 256)
        E, K = (16, 4)
        I_MOE, I_SH = (176, 704)
        key = jax.random.key(seed)
        ks = jax.random.split(key, 9)

        def w(k, shape, fan_in):
            return jax.random.normal(k, shape, jnp.float32) * fan_in ** (-0.5)
        return {'hidden_states': jax.random.normal(ks[0], (B, S, H), jnp.float32), 'router_w': w(ks[1], (E, H), H), 'w_gate': w(ks[2], (E, H, I_MOE), H), 'w_up': w(ks[3], (E, H, I_MOE), H), 'w_down': w(ks[4], (E, I_MOE, H), I_MOE), 'sh_gate': w(ks[5], (H, I_SH), H), 'sh_up': w(ks[6], (H, I_SH), H), 'sh_down': w(ks[7], (I_SH, H), I_SH), 'sh_gate_w': w(ks[8], (H, 1), H)}
    _L1_ffn_all = _L1_ffn_setup()
    _L1_ffn_in = {k: v for k, v in _L1_ffn_all.items() if k in ('router_w', 'w_gate', 'w_up', 'w_down', 'sh_gate', 'sh_up', 'sh_down', 'sh_gate_w')}
    del _L1_ffn_all
    return {'x': x, 'ctx_512': ctx_512, 'L0_attn_slope_rate': _L0_attn_in['slope_rate'], 'L0_attn_W_qkvu': _L0_attn_in['W_qkvu'], 'L0_attn_W_out': _L0_attn_in['W_out'], 'L0_xattn_W_k': _L0_xattn_in['W_k'], 'L0_xattn_b_k': _L0_xattn_in['b_k'], 'L0_xattn_ln_gamma': _L0_xattn_in['ln_gamma'], 'L0_xattn_ln_beta': _L0_xattn_in['ln_beta'], 'L0_ffn_W_router': _L0_ffn_in['W_router'], 'L0_ffn_W_gate': _L0_ffn_in['W_gate'], 'L0_ffn_W_up': _L0_ffn_in['W_up'], 'L0_ffn_W_down': _L0_ffn_in['W_down'], 'L0_ffn_sA_gate': _L0_ffn_in['sA_gate'], 'L0_ffn_sB_gate': _L0_ffn_in['sB_gate'], 'L0_ffn_sA_up': _L0_ffn_in['sA_up'], 'L0_ffn_sB_up': _L0_ffn_in['sB_up'], 'L0_ffn_sA_down': _L0_ffn_in['sA_down'], 'L0_ffn_sB_down': _L0_ffn_in['sB_down'], 'L0_ffn_A_gate': _L0_ffn_in['A_gate'], 'L0_ffn_B_gate': _L0_ffn_in['B_gate'], 'L0_ffn_A_up': _L0_ffn_in['A_up'], 'L0_ffn_B_up': _L0_ffn_in['B_up'], 'L0_ffn_A_down': _L0_ffn_in['A_down'], 'L0_ffn_B_down': _L0_ffn_in['B_down'], 'L0_ffn_expert_bias': _L0_ffn_in['expert_bias'], 'L1_attn_w_norm': _L1_attn_in['w_norm'], 'L1_attn_W_in': _L1_attn_in['W_in'], 'L1_attn_conv_w': _L1_attn_in['conv_w'], 'L1_attn_conv_b': _L1_attn_in['conv_b'], 'L1_attn_W_xp': _L1_attn_in['W_xp'], 'L1_attn_W_dt': _L1_attn_in['W_dt'], 'L1_attn_b_dt': _L1_attn_in['b_dt'], 'L1_attn_A_log': _L1_attn_in['A_log'], 'L1_attn_D': _L1_attn_in['D'], 'L1_attn_W_out': _L1_attn_in['W_out'], 'L1_ffn_router_w': _L1_ffn_in['router_w'], 'L1_ffn_w_gate': _L1_ffn_in['w_gate'], 'L1_ffn_w_up': _L1_ffn_in['w_up'], 'L1_ffn_w_down': _L1_ffn_in['w_down'], 'L1_ffn_sh_gate': _L1_ffn_in['sh_gate'], 'L1_ffn_sh_up': _L1_ffn_in['sh_up'], 'L1_ffn_sh_down': _L1_ffn_in['sh_down'], 'L1_ffn_sh_gate_w': _L1_ffn_in['sh_gate_w']}

def reference(x, ctx_512, L0_attn_slope_rate, L0_attn_W_qkvu, L0_attn_W_out, L0_xattn_W_k, L0_xattn_b_k, L0_xattn_ln_gamma, L0_xattn_ln_beta, L0_ffn_W_router, L0_ffn_W_gate, L0_ffn_W_up, L0_ffn_W_down, L0_ffn_sA_gate, L0_ffn_sB_gate, L0_ffn_sA_up, L0_ffn_sB_up, L0_ffn_sA_down, L0_ffn_sB_down, L0_ffn_A_gate, L0_ffn_B_gate, L0_ffn_A_up, L0_ffn_B_up, L0_ffn_A_down, L0_ffn_B_down, L0_ffn_expert_bias, L1_attn_w_norm, L1_attn_W_in, L1_attn_conv_w, L1_attn_conv_b, L1_attn_W_xp, L1_attn_W_dt, L1_attn_b_dt, L1_attn_A_log, L1_attn_D, L1_attn_W_out, L1_ffn_router_w, L1_ffn_w_gate, L1_ffn_w_up, L1_ffn_w_down, L1_ffn_sh_gate, L1_ffn_sh_up, L1_ffn_sh_down, L1_ffn_sh_gate_w):
    import jax
    import jax.numpy as jnp

    def _L0_attn_ref(x, slope_rate, W_qkvu, W_out):
        import jax, jax.numpy as jnp
        import numpy as np
        BLOCK = 32
        EPS = 1e-06

        def _silu(x):
            return x * jax.nn.sigmoid(x)
        b, n, embed_dim = x.shape
        h = slope_rate.shape[0]
        hidden_dim = W_qkvu.shape[0] // 4
        d = hidden_dim // h
        NB = n // BLOCK
        qkvu = x @ W_qkvu.T
        q, k, v, u = jnp.split(qkvu, 4, axis=-1)

        def to_heads(t):
            return t.reshape(b, n, h, d).transpose(0, 2, 1, 3)
        q = _silu(to_heads(q))
        k = _silu(to_heads(k))
        v = to_heads(v)
        s = slope_rate
        arr = jnp.arange(1, BLOCK + 1, dtype=x.dtype)
        q_decay = jnp.exp(-s * arr[:, None])
        k_decay = jnp.exp(-s * (BLOCK - arr[:, None]))
        idx = arr[:, None] - arr[None, :]
        diag_decay = jnp.exp(jnp.where(idx >= 0, -s * idx, -jnp.inf))
        block_decay = jnp.exp(-s * BLOCK)

        def blk(t):
            return t.reshape(b, h, NB, BLOCK, d).transpose(2, 0, 1, 3, 4)
        qb, kb, vb = (blk(q), blk(k), blk(v))

        def step(kv, inp):
            qi, ki, vi = inp
            qkv_none_diag = jnp.einsum('bhmd,bhde->bhme', qi * q_decay, kv)
            qk = jnp.einsum('bhmd,bhsd->bhms', qi, ki) * diag_decay
            qkv_diag = jnp.einsum('bhms,bhse->bhme', qk, vi)
            kv_new = block_decay * kv + jnp.einsum('bhsd,bhse->bhde', ki * k_decay, vi)
            return (kv_new, qkv_none_diag + qkv_diag)
        kv0 = jnp.zeros((b, h, d, d), dtype=jnp.float32)
        _, outs = jax.lax.scan(step, kv0, (qb, kb, vb))
        o = outs.transpose(1, 2, 0, 3, 4).reshape(b, h, n, d)
        o = o.transpose(0, 2, 1, 3).reshape(b, n, hidden_dim)
        o = o * jax.lax.rsqrt(jnp.mean(o * o, axis=-1, keepdims=True) + EPS)
        o = u * o
        return o @ W_out.T

    def _L0_xattn_ref(p, k_v, W_k, b_k, ln_gamma, ln_beta):
        import jax, jax.numpy as jnp
        import numpy as np
        EPS = 1e-06
        IMAGE_DIMS = 256
        kv = k_v @ W_k.T + b_k
        out = jnp.einsum('bij,bjd->bid', p, kv)
        scale = IMAGE_DIMS ** (-0.5)
        sim = jnp.einsum('bid,bjd->bij', out, kv) * scale
        mu = jnp.mean(sim, axis=-1, keepdims=True)
        var = jnp.var(sim, axis=-1, keepdims=True)
        sim = (sim - mu) * jax.lax.rsqrt(var + EPS) * ln_gamma + ln_beta
        attn = jax.nn.softmax(sim, axis=-1)
        return attn

    def _L0_ffn_ref(x, W_router, W_gate, W_up, W_down, sA_gate, sB_gate, sA_up, sB_up, sA_down, sB_down, A_gate, B_gate, A_up, B_up, A_down, B_down, expert_bias):
        import jax, jax.numpy as jnp
        import numpy as np
        B, L, D = (2, 128, 256)
        E, TOP_K, RANK, DFF = (8, 2, 8, 688)

        def _lora(x, A, Bm, scale):
            return x @ A @ Bm * scale

        def _expert_lora(x, A, Bm, w, scale):
            xA = jnp.einsum('bld,edr->bler', x, A)
            xAB = jnp.einsum('bler,erd->bled', xA, Bm) * scale
            return (xAB * w).sum(axis=2)
        scale = 1.0 / RANK
        logits = x @ W_router
        scores = jax.nn.sigmoid(logits)
        biased = scores + expert_bias
        _, topk_idx = jax.lax.top_k(biased, TOP_K)
        topk_scores = jnp.take_along_axis(scores, topk_idx, axis=-1)
        topk_w = topk_scores / (topk_scores.sum(-1, keepdims=True) + 1e-08)
        one_hot = jax.nn.one_hot(topk_idx, E, dtype=x.dtype)
        expert_weights = (one_hot * topk_w[..., None]).sum(axis=2)
        w = expert_weights[..., None]
        gate = x @ W_gate + _lora(x, sA_gate, sB_gate, scale) + _expert_lora(x, A_gate, B_gate, w, scale)
        up = x @ W_up + _lora(x, sA_up, sB_up, scale) + _expert_lora(x, A_up, B_up, w, scale)
        hidden = jax.nn.silu(gate) * up
        out = hidden @ W_down + _lora(hidden, sA_down, sB_down, scale) + _expert_lora(hidden, A_down, B_down, w, scale)
        return out

    def _L1_attn_ref(x, w_norm, W_in, conv_w, conv_b, W_xp, W_dt, b_dt, A_log, D, W_out):
        import jax, jax.numpy as jnp
        import numpy as np
        D_MODEL = 256
        D_INNER = 512
        D_STATE = 16
        DT_RANK = 128
        D_CONV = 4
        EPS = 1e-05

        def _rmsnorm(x, w):
            return x * jax.lax.rsqrt(jnp.mean(jnp.square(x), axis=-1, keepdims=True) + EPS) * w

        def _depthwise_causal_conv(x, conv_w, conv_b):
            k = conv_w[:, None, :]
            y = jax.lax.conv_general_dilated(x, k, window_strides=(1,), padding=((D_CONV - 1, 0),), dimension_numbers=('NWC', 'WIO', 'NWC'), feature_group_count=D_INNER)
            return y + conv_b

        def _selective_scan(u, delta, A, B, C, D):
            deltaA = jnp.exp(jnp.einsum('bld,dn->bldn', delta, A))
            deltaBu = jnp.einsum('bld,bln,bld->bldn', delta, B, u)
            dA = jnp.moveaxis(deltaA, 1, 0)
            dBu = jnp.moveaxis(deltaBu, 1, 0)
            Ct = jnp.moveaxis(C, 1, 0)
            b, l, d = u.shape
            n = A.shape[1]

            def step(h, inputs):
                dA_t, dBu_t, C_t = inputs
                h = h * dA_t + dBu_t
                y = jnp.einsum('bdn,bn->bd', h, C_t)
                return (h, y)
            h0 = jnp.zeros((b, d, n), u.dtype)
            _, ys = jax.lax.scan(step, h0, (dA, dBu, Ct))
            y = jnp.moveaxis(ys, 0, 1)
            return y + u * D
        xn = _rmsnorm(x, w_norm)
        xz = xn @ W_in
        xs, res = jnp.split(xz, 2, axis=-1)
        xs = _depthwise_causal_conv(xs, conv_w, conv_b)
        xs = jax.nn.silu(xs)
        A = -jnp.exp(A_log)
        xdbc = xs @ W_xp
        dt_r = xdbc[..., :DT_RANK]
        B = xdbc[..., DT_RANK:DT_RANK + D_STATE]
        C = xdbc[..., DT_RANK + D_STATE:]
        delta = jax.nn.softplus(dt_r @ W_dt + b_dt)
        y = _selective_scan(xs, delta, A, B, C, D)
        y = y * jax.nn.silu(res)
        out = y @ W_out + x
        return out

    def _L1_xattn_ref(q, k, v):
        import jax, jax.numpy as jnp
        import numpy as np
        import math
        NUM_Q_HEADS = 32
        NUM_KV_HEADS = 8
        B, S, E = q.shape
        H, KV = (NUM_Q_HEADS, NUM_KV_HEADS)
        D = E // H
        G = H // KV
        scale = math.sqrt(D)
        qh = q.reshape(B, S, KV, G, D).transpose(0, 2, 3, 1, 4)
        kh = k.reshape(B, S, KV, D).transpose(0, 2, 1, 3)
        vh = v.reshape(B, S, KV, D).transpose(0, 2, 1, 3)
        scores = jnp.einsum('bkgsd,bktd->bkgst', qh, kh) / scale
        weights = jax.nn.softmax(scores, axis=-1)
        out = jnp.einsum('bkgst,bktd->bkgsd', weights, vh)
        return out.transpose(0, 3, 1, 2, 4).reshape(B, S, E)

    def _L1_ffn_ref(hidden_states, router_w, w_gate, w_up, w_down, sh_gate, sh_up, sh_down, sh_gate_w):
        import jax, jax.numpy as jnp
        import numpy as np
        B, S, H = (2, 256, 256)
        E, K = (16, 4)
        I_MOE, I_SH = (176, 704)
        orig = hidden_states.shape
        h = hidden_states.reshape(-1, orig[-1])
        N = h.shape[0]
        logits = h @ router_w.T
        probs = jax.nn.softmax(logits.astype(jnp.float32), axis=-1)
        top_vals, top_idx = jax.lax.top_k(probs, K)
        top_vals = top_vals / jnp.maximum(top_vals.sum(-1, keepdims=True), 1e-09)
        top_vals = top_vals.astype(h.dtype)
        comb = jnp.zeros((N, E), h.dtype).at[jnp.arange(N)[:, None], top_idx].add(top_vals)
        g = jnp.einsum('nh,ehi->eni', h, w_gate)
        u = jnp.einsum('nh,ehi->eni', h, w_up)
        y = jnp.einsum('eni,eih->enh', jax.nn.silu(g) * u, w_down)
        routed = jnp.einsum('enh,ne->nh', y, comb)
        shared = jax.nn.silu(h @ sh_gate) * (h @ sh_up) @ sh_down
        sg = jax.nn.sigmoid(h @ sh_gate_w)
        return (routed + sg * shared).reshape(orig)
    x = _layernorm(x + _L0_attn_ref(x, L0_attn_slope_rate, L0_attn_W_qkvu, L0_attn_W_out), axis=-1)
    x = _layernorm(x + _L0_xattn_ref(x, ctx_512, L0_xattn_W_k, L0_xattn_b_k, L0_xattn_ln_gamma, L0_xattn_ln_beta), axis=-1)
    x = _layernorm(x + _L0_ffn_ref(x, L0_ffn_W_router, L0_ffn_W_gate, L0_ffn_W_up, L0_ffn_W_down, L0_ffn_sA_gate, L0_ffn_sB_gate, L0_ffn_sA_up, L0_ffn_sB_up, L0_ffn_sA_down, L0_ffn_sB_down, L0_ffn_A_gate, L0_ffn_B_gate, L0_ffn_A_up, L0_ffn_B_up, L0_ffn_A_down, L0_ffn_B_down, L0_ffn_expert_bias), axis=-1)
    x = _layernorm(x + _L1_attn_ref(x, L1_attn_w_norm, L1_attn_W_in, L1_attn_conv_w, L1_attn_conv_b, L1_attn_W_xp, L1_attn_W_dt, L1_attn_b_dt, L1_attn_A_log, L1_attn_D, L1_attn_W_out), axis=-1)
    x = _layernorm(x + _L1_xattn_ref(x, ctx_512, ctx_512), axis=-1)
    x = _layernorm(x + _L1_ffn_ref(x, L1_ffn_router_w, L1_ffn_w_gate, L1_ffn_w_up, L1_ffn_w_down, L1_ffn_sh_gate, L1_ffn_sh_up, L1_ffn_sh_down, L1_ffn_sh_gate_w), axis=-1)
    return x

_drawn_inputs = setup_inputs


def setup_inputs(seed=0):
    import zlib

    import numpy as np

    out = dict(_drawn_inputs(seed))
    spreads = {'L0_xattn_b_k': (0.0, 0.8),
     'L0_xattn_ln_gamma': (1.0, 0.6),
     'L0_xattn_ln_beta': (0.0, 0.8),
     'L0_ffn_expert_bias': (0.0, 0.8),
     'L1_attn_w_norm': (1.0, 0.6),
     'L1_attn_conv_b': (0.0, 0.8),
     'L1_attn_b_dt': (-4.0, 0.6),
     'L1_attn_D': (1.0, 0.6)}
    factors = {'L0_xattn_W_k': 4.667,
     'L0_ffn_W_router': 4.452,
     'L0_ffn_sA_gate': 6.543,
     'L0_ffn_sB_gate': 5.723,
     'L0_ffn_sA_up': 6.507,
     'L0_ffn_sB_up': 5.637,
     'L0_ffn_sA_down': 6.01,
     'L0_ffn_sB_down': 5.679,
     'L0_ffn_A_gate': 6.313,
     'L0_ffn_B_gate': 5.617,
     'L0_ffn_A_up': 6.423,
     'L0_ffn_B_up': 5.526,
     'L0_ffn_A_down': 5.954,
     'L0_ffn_B_down': 6.864,
     'L1_attn_W_in': 4.477,
     'L1_attn_conv_w': 4.841,
     'L1_attn_W_xp': 8.0,
     'L1_attn_W_dt': 8.0,
     'L1_attn_A_log': 8.0,
     'L1_attn_W_out': 4.588}
    for name, (base, spread) in spreads.items():
        noise = np.random.default_rng([zlib.crc32(name.encode()), seed]).standard_normal(out[name].shape)
        drawn = base * np.exp(spread * noise) if base else spread * noise
        out[name] = jnp.asarray(drawn.astype(out[name].dtype))
    for name, factor in factors.items():
        out[name] = (out[name] * factor).astype(out[name].dtype)
    return out
```

```python
from contextlib import ExitStack

import concourse.bass as bass
from concourse import mybir

F32 = mybir.dt.float32
BF16 = mybir.dt.bfloat16
ALU = mybir.AluOpType
ACT = mybir.ActivationFunctionType
AX_X = mybir.AxisListType.X

P = 128
B, S, D = 4, 256, 256
TT, KT = S // P, D // P
H0, HD0 = 16, 16
CD = 64
E0, RANK, DFF = 8, 8, 688
E0S = E0 + 1
LR = E0S * RANK
MT0 = -(-DFF // P)
DI, NS, DTR, NCONV = 512, 16, 128, 4
DT = DI // P
NG = 4
NSTEP = NS // NG * DT
HQ, HKV, HD1 = 32, 8, 8
HG = HQ // HKV
E1, TOP1, IE, ISH = 16, 4, 176, 704
MTE = E1 * IE // P
MTS = -(-ISH // P)
MT1 = MTE + MTS
MW_RING = 5
NEG = -1e30

C_IDENT, C_DIST, C_CAUSAL, C_HEADMASK, C_PARTID, C_END = 0, 128, 384, 640, 648, 680
V_WN, V_CW, V_CB, V_BDT, V_D, V_ALOG, V_BK, V_BCS, V_END = 0, 2, 18, 22, 26, 30, 94, 95, 96
R_GAMMA, R_BETA, R_BK, R_EB, R_SLOPE, R_END = 0, 256, 512, 576, 584, 600

PAIRS = [f"at{i}" for i in range(H0 // 2)]
FFN_G = [f"fg{m}" for m in range(MT0)]
STEPS = [f"s{n}" for n in range(NSTEP)]
BMAX = [f"bm{i}" for i in range(HQ // 2)]
BG = [f"bg{g}{c}" for g in range(HKV) for c in "ab"]
BE = [f"be{m}" for m in range(MT1)]
FRONT = (["load", "qkv"] + PAIRS + ["oa", "ob", "xa", "xb", "xc", "xd", "fa1", "fa2", "fa3"] + FFN_G +
         ["fd1", "fd2", "fd3", "m1", "m2", "m3", "m4", "m5", "d1", "d2", "d3", "d4"] + STEPS + ["u1", "u2"])
BACK = ["bq1", "bq2", "bq3"] + BMAX + BG + ["ba1", "ba2", "br1", "br2", "br3"] + BE + ["bout"]
AFTER = {"load": 2, "qkv": 1, "at0": 1, "at1": 1, "at2": 2, "at3": 2, "at5": 3, "at6": 2, "at7": 3, "oa": 2, "ob":
         2, "xa": 1, "xb": 2, "xc": 4, "xd": 3, "fa1": 1, "fa2": 1, "fa3": 2, "fg0": 1, "fg1": 1, "fg2": 1, "fg3":
         1, "fg4": 1, "fg5": 2, "fd1": 1, "fd2": 1, "fd3": 1, "m1": 1, "m2": 2, "m5": 2, "d1": 1, "d2": 2, "d3": 2,
         "d4": 1, "s0": 1, "s1": 1, "s2": 1, "s3": 1, "s4": 1, "s5": 1, "s6": 1, "s7": 1, "s8": 1, "s9": 1, "s11":
         2, "s15": 1}
AFTER_PE = {"load": 2, "qkv": 1, "at0": 1, "at1": 2, "at2": 2, "at3": 1, "at5": 3, "at6": 2, "at7": 3, "oa": 2,
            "ob": 2, "xa": 1, "xb": 2, "xc": 4, "xd": 3, "fa1": 2, "fa3": 2, "fg0": 1, "fg1": 1, "fg2": 1, "fg3": 1,
            "fg4": 1, "fg5": 2, "fd1": 1, "fd2": 1, "fd3": 1, "m1": 1, "m2": 2, "m5": 2, "d1": 1, "d2": 2, "d3": 2,
            "d4": 1, "s0": 1, "s1": 1, "s2": 1, "s3": 1, "s4": 1, "s5": 1, "s6": 1, "s7": 1, "s8": 1, "s9": 1,
            "s10": 1, "s11": 1, "s15": 1}
AFTER_DVE = {"load": 2, "qkv": 1, "at0": 1, "at1": 1, "at2": 2, "at3": 2, "at5": 3, "at6": 2, "at7": 3, "oa": 2,
             "ob": 2, "xa": 1, "xb": 2, "xc": 4, "xd": 3, "fa1": 1, "fa2": 1, "fa3": 2, "fg0": 1, "fg1": 1, "fg2":
             1, "fg3": 1, "fg4": 1, "fg5": 2, "fd1": 1, "fd2": 1, "fd3": 1, "m1": 1, "m2": 2, "m5": 2, "d1": 1,
             "d2": 2, "d3": 2, "d4": 1, "s0": 1, "s1": 1, "s2": 1, "s3": 1, "s4": 1, "s5": 1, "s6": 1, "s7": 1,
             "s8": 1, "s9": 1, "s11": 2, "s15": 1}


def merged(after):
    assert sum(after.values()) == len(BACK)
    back, out = iter(BACK), []
    for ph in FRONT:
        out += [("F", ph)] + [("B", next(back)) for _ in range(after.get(ph, 0))]
    return out


class Steps:

    def __init__(self, sem, known, ahead):
        self.sem, self.known, self.ahead = sem, known, ahead
        self.number, self.count, self.seen = {}, 0, 0
        self.total = known["total"] if known else 1
        self.base = self.total * ahead

    def begin(self):
        if self.count:
            assert self.count == self.seen or not self.seen
            self.seen = self.count
        self.count = 0

    def step(self, name=None):
        self.count += 1
        if name is not None:
            self.number[name] = self.count
        return self.sem

    def at(self, name, b):
        number = self.known["number"][name] if self.known else 1
        return self.sem, b * self.total + (number + self.base)

    def last(self, b):
        return self.sem, b * self.total + (self.count + self.base)

    def end(self, b):
        return self.sem, b * self.total + (self.total + self.base)


def build(nc, ins, out, known):
    ctx = ExitStack()
    with ctx:
        def sb(name, shape, dt=F32):
            return ctx.enter_context(nc.sbuf_tensor(name, shape, dt))

        def sem(name):
            return ctx.enter_context(nc.semaphore(name))

        FA = E0 + 2 * LR
        FDN = D + LR
        room = sb("room", [P, 2 * KT * MT0 * P + MT0 * FDN + KT * FA])
        w_l0 = room[:, 0:KT * 4 * D + KT * D]
        wqkvu = w_l0[:, 0:KT * 4 * D].rearrange("p (k n) -> p k n", k=KT)
        wo0 = w_l0[:, KT * 4 * D:].rearrange("p (k n) -> p k n", k=KT)
        wk = sb("wk", [CD, CD])
        w_f = room[:, :]
        o1, o2 = KT * MT0 * P, 2 * KT * MT0 * P
        o3 = o2 + MT0 * FDN
        wgate = w_f[:, 0:o1].rearrange("p (k n) -> p k n", k=KT)
        wup = w_f[:, o1:o2].rearrange("p (k n) -> p k n", k=KT)
        wdown = w_f[:, o2:o3].rearrange("p (k n) -> p k n", k=MT0)
        wrouter0 = w_f[:, o3:].rearrange("p (k n) -> p k n", k=KT)
        w_lb = sb("w_lb", [LR, 2 * MT0 * P + D])
        bgate, bup, bdown = w_lb[:, 0:MT0 * P], w_lb[:, MT0 * P:2 * MT0 * P], w_lb[:, 2 * MT0 * P:]
        w_m = sb("w_m", [P, KT * 2 * DI + DT * (DTR + 2 * NS) + DI + DT * D])
        m1 = KT * 2 * DI
        m2 = m1 + DT * (DTR + 2 * NS)
        m3 = m2 + DI
        win = w_m[:, 0:m1].rearrange("p (k n) -> p k n", k=KT)
        wxp = w_m[:, m1:m2].rearrange("p (k n) -> p k n", k=DT)
        wdt = w_m[:, m2:m3]
        wmo = w_m[:, m3:].rearrange("p (k n) -> p k n", k=DT)
        wr1 = sb("wr1", [P, KT, E1 + 1])
        mw = sb("mw", [P, MW_RING, 3 * D])
        ident = sb("ident", [P, P])
        ident_bf = sb("ident_bf", [P, P], BF16)
        pick = sb("pick", [P, 32], BF16)
        headmask = sb("headmask", [P, 8])
        ones = sb("ones", [P, 1])
        minus_half = sb("minus_half", [P, 2])
        idle_v, idle_g = sb("idle_v", [P, 1]), sb("idle_g", [P, 1])
        vec = sb("vec", [P, V_END])
        a_neg = sb("a_neg", [P, DT * NS])
        d_half = sb("d_half", [P, DT])
        rows = sb("rows", [P, R_END])
        decay = sb("decay", [P, H0, S])
        expand = sb("expand", [P, MT1 * P], BF16)

        x_tok = sb("x_tok", [P, TT, D])
        x_t = sb("x_t", [P, KT, S])
        ctx_t = sb("ctx_t", [CD, S])
        kv_t = sb("kv_t", [CD, S])
        kv = sb("kv", [P, TT, CD])
        o_t = sb("o_t", [CD, S])
        vz = sb("vz", [P, TT, H0, 32])
        xp = sb("xp", [P, TT, D])
        xa = sb("xa", [P, TT, D])
        xb = sb("xb", [P, TT, D])
        xt = sb("xt", [P, KT, S])
        st6 = sb("st6", [P, TT, 6])
        mv = sb("mv", [P, TT, 2])
        ve = sb("ve", [P, TT])
        rs = sb("rs", [P, TT])
        small = sb("small", [P, 16])
        lg0 = sb("lg0", [P, TT, E0])
        sc0 = sb("sc0", [P, TT, E0])
        bi0 = sb("bi0", [P, TT, 16])
        rp0 = sb("rp0", [P, TT, 16])
        v80 = sb("v80", [P, TT, 8])
        tr0 = sb("tr0", [P, TT, 8])
        w9 = sb("w9", [P, TT, E0S])
        zz = sb("zz", [P, TT, 2 * LR])
        z_t = sb("z_t", [LR, 2, S])
        u2 = sb("u2", [P, DT, S])
        sres = sb("sres", [P, DT, S])
        delta = sb("delta", [P, DT, S])
        du = sb("du", [P, DT, S])
        dtr = sb("dtr", [P, S])
        bct = sb("bct", [32, S])
        bcr = sb("bcr", [32, S])
        bcm = sb("bcm", [32, S], BF16)
        bcp = sb("bcp", [P, S], BF16)
        arena = sb("arena", [P, 8192 + 2048])
        kz = arena[:, 0:4096].rearrange("p (f v t) -> p f v t", f=KT, v=8)
        A_RING = 6
        att = arena[:, 4096:4096 + A_RING * 384].rearrange("p (r n) -> p r n", r=A_RING)
        qs = arena[:, 6400:6912]
        ks = arena[:, 6912:7424]
        us = arena[:, 7424:7936]
        th_a = arena[:, 7936:8448]
        th_b = arena[:, 8448:8960]
        osq, uo = arena[:, 8960:9472], arena[:, 9472:9984]
        en = arena[:, 0:512].rearrange("p (t n) -> p t n", t=TT)
        ee = arena[:, 512:1024].rearrange("p (t n) -> p t n", t=TT)
        hid0 = arena[:, 1024:1024 + MT0 * S].rearrange("p (m n) -> p m n", m=MT0)
        tf = arena[:, 2560:3072].rearrange("p (r n) -> p r n", r=2)
        ta = arena[:, 3072:3584].rearrange("p (r n) -> p r n", r=2)
        zd = arena[:, 3584:3584 + TT * LR].rearrange("p (t n) -> p t n", t=TT)
        zd_t = arena[0:LR, 3840:3840 + S]
        sqj = arena[:, 4096:4608].rearrange("p (t n) -> p t n", t=TT)
        CW = S + NCONV - 1
        xc = arena[:, 4608:4608 + DT * CW].rearrange("p (d n) -> p d n", d=DT)
        acc = arena[:, 5664:6688]
        th_c = arena[:, 6688:7712]
        th_u = arena[:, 7712:8736]
        e1 = arena[:, 4096:5120]
        t_w = arena[:, 5120:6144]
        t_ln = arena[:, 6144:7168]
        t_rz = arena[:, 7168:8192]
        hb = arena[:, 0:4096].rearrange("p (r n) -> p r n", r=4)
        rep = arena[:, 6144:6144 + 4096].rearrange("p (g c n) -> p g c n", g=2, c=2)
        dA = arena[:, 4096:6144].rearrange("p (r s n) -> p r s n", r=2, s=NG)
        yz = arena[:, 0:1024].rearrange("p (d n) -> p d n", d=DT)

        x4 = sb("x4", [P, TT, D])
        x5 = sb("x5", [P, TT, D])
        xq = sb("xq", [P, TT, D])
        c_tok = sb("c_tok", [P, TT, CD])
        kr = sb("kr", [P, TT, CD])
        v32 = sb("v32", [P, TT, HKV, 32])
        big = sb("big", [P, 4096], BF16)
        q_sl = big[:, 0:4096].rearrange("p (t h n) -> p (t h) n", t=TT, h=HQ)
        q_tr = big[:, 0:4096].rearrange("p (t h n) -> p t h n", t=TT, h=HQ // 2)
        k_sl = big[:, :].rearrange("p (n v w) -> p n v w", v=2, w=P)
        k_tr = big[:, :].rearrange("p (t n w) -> p t n w", t=TT, w=P)
        probs = big[:, :].bitcast(F32).rearrange("p (r n) -> p r n", r=4)
        q_t = sb("q_t", [P, HQ // 2, S], BF16)
        k_t = sb("k_t", [P, HKV, 2, S], BF16)
        ao = q_t[:, :, :].rearrange("p h t -> p (h t)").bitcast(F32).rearrange("p (g t) -> p g t", g=HKV)
        nmx = sb("nmx", [P, TT, HQ])
        nmb = sb("nmb", [P, TT, HQ], BF16)
        nm_t = sb("nm_t", [P, S], BF16)
        rec = sb("rec", [P, 4, 16])
        st6b = sb("st6b", [P, TT, 6])
        mvb = sb("mvb", [P, TT, 2])
        veb = sb("veb", [P, TT])
        rsb = sb("rsb", [P, TT])
        smb = sb("smb", [P, 16])
        lg1 = sb("lg1", [P, TT, E1 + 1])
        pr1 = sb("pr1", [P, TT, E1 + 8])
        rp1 = sb("rp1", [P, TT, E1 + 8])
        v81 = sb("v81", [P, TT, 8])
        tr1 = sb("tr1", [P, TT, 8])
        cb = sb("cb", [P, TT, 32])
        cbr = sb("cbr", [P, TT, 32])
        cp = sb("cp", [P, TT, 96], BF16)
        c_t = sb("c_t", [P, S], BF16)
        crs = ao[:, 0:4, :].rearrange("p (r m) n -> p r m n", r=2)
        thg, hraw = ao[:, 4:6, :], ao[:, 6:8, :]
        spare = k_t[:, :, :, :].rearrange("p g v t -> p (g v t)").bitcast(F32)
        x5t = spare[:, 0:KT * S].rearrange("p (k t) -> p k t", k=KT)
        hid1 = spare[:, KT * S:(KT + 3) * S].rearrange("p (r t) -> p r t", r=3)

        F = [ctx.enter_context(nc.psum_tensor(f"F{i}", [P, 512], F32)) for i in range(4)]
        K = [ctx.enter_context(nc.psum_tensor(f"B{i}", [P, 512], F32)) for i in range(4)]

        def two(bank):
            return bank[:, :].rearrange("p (t n) -> p t n", t=2)

        def halfword(bank):
            return bank[:, :].bitcast(BF16)

        names = ["pe_front", "act_front", "dve_front", "pool_front", "pe_back", "act_back", "dve_back", "pool_back"]
        steps = {n: Steps(sem(n), known.get(n), n.endswith("back")) for n in names}
        pf, af, df, gf, pb, ab, db, gb = (steps[n] for n in names)
        consts_in = sem("consts_in")
        weights_in = sem("weights_in")
        l0_in, f_in = sem("l0_in"), sem("f_in")
        x_in = sem("x_in")
        c_in = sem("c_in")
        mw_in = [sem(f"mw_in{i}") for i in range(MW_RING)]
        out_done = sem("out_done")
        init = sem("init")
        expand_filled = sem("expand_filled")
        init_v = sem("init_v")
        init_a = sem("init_a")
        N_INIT, N_INIT_V, N_INIT_A = 14, 6, 17

        ORDER, ORDER_PE, ORDER_DVE = merged(AFTER), merged(AFTER_PE), merged(AFTER_DVE)
        block = ctx.enter_context(nc.Block())

        def run(eng, front, back, begin_f, begin_b, order):
            def fresh():
                for n in begin_f + begin_b:
                    n.begin()
            for ph in FRONT:
                front(0, ph)
            with eng.Fori(1, B) as b:
                fresh()
                for stream, ph in order:
                    (front if stream == "F" else back)(b if stream == "F" else b - 1, ph)
            fresh()
            for ph in BACK:
                back(B - 1, ph)
            fresh()

        def head(n):
            q, j = divmod(n, 4)
            return 8 * (q // 2) + 2 * j + q % 2

        def in_pairs(b, n):
            return later(b) and n < NSTEP - DT

        def later(b):
            return not (isinstance(b, int) and b == 0)


        @block.sync
        def _(sp):
            sp.dma_start(arena[:, 0:C_END], ins["consts"]).then_inc(consts_in, 16)
            sp.dma_start(rows[:, :], ins["rows"]).then_inc(consts_in, 16)
            sp.dma_start(vec[:, :], ins["vec"]).then_inc(consts_in, 16)
            sp.dma_start(wk[:, :], ins["wk"]).then_inc(consts_in, 16)

            def load(b):
                row = bass.ds(b, 1)
                sp.dma_start(w_l0, ins["w_l0"]).then_inc(l0_in, 16)
                sp.dma_start(x_tok[:, :, :], ins["x_tok"][row].rearrange("o p t n -> p (o t) n")).then_inc(x_in, 16)
                sp.dma_start(x_t[:, :, :], ins["x_t"][row].rearrange("o p t n -> p (o t) n")).then_inc(x_in, 16)
                sp.dma_start(ctx_t[:, :], ins["ctx_t"][row].rearrange("o p n -> (o p) n")).then_inc(x_in, 16)

            def front(b, ph):
                if ph == "ob":
                    sp.wait_ge(*pf.at("wo", b))
                    sp.dma_start(w_f, ins["w_f"]).then_inc(f_in, 16)
                    if later(b):
                        sp.wait_ge(*gf.at("k_split", b - 1))
                    sp.dma_start(c_tok[:, :, :], ins["c_tok"][bass.ds(b, 1)].rearrange("o p t n -> p (o t) n"))\
                        .then_inc(c_in, 16)
                if ph == "m5" and not (isinstance(b, int) and b == B - 1):
                    sp.wait_ge(*pf.at("down", b))
                    sp.wait_ge(*df.at("x_tok_read", b))
                    load(b + 1)

            def back(b, ph):
                if ph == "bq1":
                    sp.wait_ge(*pb.at(f"down{MT1 - 1}", b - 1))
                    for m in range(MW_RING):
                        sp.dma_start(mw[:, m, :], ins["w_moe"][m]).then_inc(mw_in[m], 16)
                if ph in BE and BE.index(ph) + MW_RING < MT1:
                    m = BE.index(ph)
                    sp.wait_ge(*pb.at(f"down{m}", b))
                    sp.dma_start(mw[:, m % MW_RING, :], ins["w_moe"][m + MW_RING])\
                        .then_inc(mw_in[m % MW_RING], 16)
                if ph == "bout":
                    sp.wait_ge(*db.at("y", b))
                    sp.dma_start(out[bass.ds(b, 1)].rearrange("o (t p) n -> p (o t) n", p=P), x5[:, :, :])\
                        .then_inc(out_done, 16)

            load(0)
            sp.dma_start(w_lb[:, :], ins["w_lb"]).then_inc(weights_in, 16)
            sp.dma_start(w_m[:, :], ins["w_m"]).then_inc(weights_in, 16)
            sp.dma_start(wr1[:, :, :], ins["wr1"]).then_inc(weights_in, 16)
            for ph in FRONT:
                front(0, ph)
            with sp.Fori(1, B - 1) as b:
                for stream, ph in ORDER:
                    (front if stream == "F" else back)(b if stream == "F" else b - 1, ph)
            for stream, ph in ORDER:
                (front if stream == "F" else back)(B - 1 if stream == "F" else B - 2, ph)
            for ph in BACK:
                back(B - 1, ph)
            sp.wait_ge(out_done, 16 * B)

        @block.gpsimd
        def _(pool):
            g = nc.gpsimd
            g.memset(vz[:, :, :, :], 0.0).then_inc(init, 1)
            g.memset(ones[:, :], 1.0).then_inc(init, 1)
            g.memset(minus_half[:, :], -0.5).then_inc(init, 1)
            g.memset(bi0[:, :, :], NEG).then_inc(init, 1)
            g.memset(tr0[:, :, :], NEG).then_inc(init, 1)
            g.memset(pr1[:, :, :], -1.0).then_inc(init, 1)
            g.memset(tr1[:, :, :], -1.0).then_inc(init, 1)
            g.memset(w9[:, :, :], 1.0 / RANK).then_inc(init, 1)
            g.memset(cb[:, :, :], 0.0).then_inc(init, 1)
            g.memset(v32[:, :, :, :], 0.0).then_inc(init, 1)
            pool.wait_ge(init, 10)
            g.memset(v32[:, :, :, HD1:HD1 + 1], 1.0).then_inc(init, 1)
            for t in (bcp, nm_t, c_t):
                g.memset(t[:, :], 0.0).then_inc(init, 1)

            pool.wait_ge(init, N_INIT)
            for i, s_ in enumerate((pb, gb, db, ab)):
                g.memset(x4[:, 0, i:i + 1], 0.0).then_inc(s_.sem, s_.total)

            def fill_expand():
                g.memset(expand[:, :], 0.5).then_inc(expand_filled, 1)
                for k in range(3):
                    r = slice(32 * k, 32 * k + 32)
                    n = E1 * IE
                    pool.wait_ge(expand_filled, 1 + 3 * k)
                    g.affine_select(out=expand[r, 0:n], in_=expand[r, 0:n], compare_op=ALU.is_ge, fill=0.0, base=0,
                                    pattern=[[1, n]], channel_multiplier=-IE).then_inc(expand_filled, 1)
                    pool.wait_ge(expand_filled, 2 + 3 * k)
                    g.affine_select(out=expand[r, 0:n], in_=expand[r, 0:n], compare_op=ALU.is_ge, fill=0.0,
                                    base=IE - 1, pattern=[[-1, n]], channel_multiplier=IE).then_inc(expand_filled, 1)
                    g.affine_select(out=expand[r, n:], in_=expand[r, n:], compare_op=ALU.is_equal, fill=0.0,
                                    base=-E1, pattern=[[0, MT1 * P - n]], channel_multiplier=1)\
                        .then_inc(expand_filled, 1)
                pool.wait_ge(expand_filled, 10)

            def settle():
                g.tensor_tensor(idle_g[:, :], ones[:, :], ones[:, :], ALU.mult).then_inc(gf.step(), 1)

            def rsqrt(dst, src, wait, steps_, name):
                pool.wait_ge(*wait)
                g.tensor_tensor(dst[:, :], src[:, :], minus_half[:, :], ALU.pow).then_inc(steps_.step(name), 1)

            def scan_input(b, n):
                ng, d = divmod(n, DT)
                pool.wait_ge(*af.at(f"rep{ng}_1", b))
                if n == 0:
                    pool.wait_ge(*df.at("du", b))
                if n >= 4:
                    pool.wait_ge(*pf.at(f"y{n - 4}", b))
                g.tensor_tensor(hb[:, n % 4, :].rearrange("p (s t) -> p s t", s=NG),
                                du[:, d, :].unsqueeze(1).to_broadcast([P, NG, S]),
                                rep[:, ng % 2, 0, :].rearrange("p (s t) -> p s t", s=NG), ALU.mult)\
                    .then_inc(gf.step(f"dbu{n}"), 1)

            def front(b, ph):
                if ph in PAIRS:
                    n = 2 * PAIRS.index(ph) + 1
                    h = head(n)
                    if n == 1 and not later(b):
                        pool.wait_ge(init_v, N_INIT_V)
                    pool.wait_ge(*af.at(f"c{n}", b))
                    a_ = att[:, n % A_RING, :]
                    g.tensor_tensor(a_[:, 0:S], a_[:, 0:S], decay[:, h, :], ALU.mult).then_inc(gf.step(), 1)
                    g.tensor_tensor(a_[:, S:S + P], a_[:, S:S + P], decay[:, h, 0:P], ALU.mult)\
                        .then_inc(gf.step(f"a{n}"), 1)
                if ph == "ob":
                    rsqrt(rs, ve, df.at("ve_o", b), gf, "rs_o")
                    rsqrt(rs, ve, df.at("ve_ln1", b), gf, "rs_ln1")
                if ph == "xc":
                    rsqrt(rs, ve, df.at("ve_sim", b), gf, "rs_sim")
                if ph == "fa1" and not later(b):
                    fill_expand()
                if ph == "xd":
                    rsqrt(rs, ve, df.at("ve_ln2", b), gf, "rs_ln2")
                if ph == "fd3":
                    rsqrt(rs, ve, df.at("ve_ln3", b), gf, "rs_ln3")
                if ph == "m1":
                    rsqrt(rs, ve, df.at("ve_rms", b), gf, "rs_rms")
                if ph == "m2":
                    pool.wait_ge(*pb.at("av7", b - 1))
                    pool.wait_ge(c_in, b * 16 + 16)
                    settle()
                    g.memset(big[:, :], 0.0).then_inc(gf.step("zero_k"), 1)
                    g.tensor_copy(v32[:, :, :, 0:HD1], c_tok[:, :, :].rearrange("p t (g d) -> p t g d", d=HD1))\
                        .then_inc(gf.step("v32"), 1)
                    flat = c_tok[:, :, :].rearrange("p t c -> p (t c)")
                    krf = kr[:, :, :].rearrange("p t c -> p (t c)")
                    kr3 = kr[:, :, :].rearrange("p t (g d) -> p (t g) d", d=HD1)
                    g.tensor_scalar(krf, flat, float(HD1) ** -0.5, None, ALU.mult).then_inc(gf.step(), 1)

                    def slot(v, j):
                        return k_sl[:, :, v, v * 64 + 8 * j:v * 64 + 8 * j + 8]

                    for part, slots in enumerate(((0, 2, 5), (1, 3), (4,))):
                        pool.wait_ge(*gf.last(b))
                        settle()
                        g.tensor_copy(slot(0, slots[0]), kr3).then_inc(gf.step(), 1)
                        pool.wait_ge(*gf.last(b))
                        settle()
                        for v in range(2):
                            for j in slots[1 - v:]:
                                ins_ = g.tensor_copy(slot(v, j), slot(0, slots[0]))
                                ins_.then_inc(gf.step("k_split" if part == 2 else None), 1)
                        if part < 2:
                            g.tensor_tensor(kr3, kr3, slot(0, slots[0]), ALU.subtract).then_inc(gf.step(), 1)
                if ph == "d4":
                    scan_input(b, 0)
                    scan_input(b, 1)
                if ph in STEPS[:-2]:
                    scan_input(b, STEPS.index(ph) + 2)
                if ph == "u2":
                    rsqrt(rs, ve, df.at("ve_ln4", b), gf, "rs_ln4")

            def back(b, ph):
                if ph == "ba2":
                    rsqrt(rsb, veb, db.at("ve_ln5", b), gb, "rs_ln5")
                if ph in BE:
                    m = BE.index(ph)
                    pool.wait_ge(*ab.at(f"cr{m // 2}", b))
                    pool.wait_ge(*db.at(f"gu{m}", b))
                    if m >= 3:
                        pool.wait_ge(*pb.at(f"down{m - 3}", b))
                    g.tensor_tensor(hid1[:, m % 3, :], hraw[:, m % 2, :], crs[:, (m // 2) % 2, m % 2, :], ALU.mult)\
                        .then_inc(gb.step(f"hid{m}"), 1)
                if ph == "bout":
                    rsqrt(rsb, veb, db.at("ve_ln6", b), gb, "rs_ln6")

            run(pool, front, back, [gf], [gb], ORDER)

        @block.scalar
        def _(act):
            a = nc.scalar
            act.wait_ge(consts_in, 64)
            a.activation(a_neg[:, :], vec[:, V_ALOG:V_ALOG + DT * NS], ACT.Exp).then_inc(init_a, 1)
            act.wait_ge(init_v, 4)
            for h in range(H0):
                a.activation(decay[:, h, :], arena[:, C_DIST:C_DIST + S], ACT.Exp,
                             scale=rows[:, R_SLOPE + h:R_SLOPE + h + 1]).then_inc(init_a, 1)

            def copy(dst, src, steps_, name, **kw):
                a.activation(dst, src, ACT.Copy, **kw).then_inc(steps_.step(name), 1)

            def front(b, ph):
                if ph == "qkv":
                    if not later(b):
                        act.wait_ge(init, 1)
                    else:
                        act.wait_ge(*df.at("yz1", b - 1))
                    act.wait_ge(*pf.at("q", b))
                    a.activation(th_a, F[1][:, :], ACT.Tanh, scale=0.5).then_inc(af.step("th_q"), 1)
                    act.wait_ge(*pf.at("k", b))
                    a.activation(th_b, F[2][:, :], ACT.Tanh, scale=0.5).then_inc(af.step("th_k"), 1)
                    act.wait_ge(*pf.at("u", b))
                    copy(us, F[3][:, :], af, "us")
                    act.wait_ge(*pf.at("v", b))
                    v = F[0][:, :].rearrange("p (t h c d) -> p t h c d", t=TT, c=2, d=HD0)
                    z = vz[:, :, :, :].rearrange("p t (h c) n -> p t h c n", c=2)
                    for c in range(2):
                        copy(z[:, :, :, c, c * HD0:c * HD0 + HD0], v[:, :, :, c, :], af, f"vz{c}")
                if ph in PAIRS:
                    n = 2 * PAIRS.index(ph) + 1
                    if n >= A_RING:
                        act.wait_ge(*pf.at(f"av{(n - A_RING) // 4}", b))
                    act.wait_ge(*pf.at(f"s{n}", b))
                    copy(att[:, n % A_RING, :], F[n % 3][:, 0:S + P], af, f"c{n}")
                if ph == "oa":
                    act.wait_ge(*pf.at("av3", b))
                    a.activation(osq, F[3][:, :], ACT.Square).then_inc(af.step("osq"), 1)
                    act.wait_ge(*pf.at("kv_t", b))
                    a.activation(kv_t[:, :], F[1][0:CD, 0:S], ACT.Identity, bias=vec[0:CD, V_BK:V_BK + 1])\
                        .then_inc(af.step("kv_t"), 1)
                if ph == "xa":
                    act.wait_ge(*pf.at("x1t", b))
                    copy(xt[:, :, :], two(F[0]), af, "x1t")
                if ph == "xb":
                    act.wait_ge(*pf.at("o_t", b))
                    copy(o_t[:, :], F[3][0:CD, 0:S], af, "o_t")
                if ph == "xd":
                    act.wait_ge(*df.at("nmx", b))
                    for t in range(TT):
                        a.activation(ee[:, t, :], en[:, t, :], ACT.Exp, bias=small[:, t:t + 1],
                                     accum_out=small[:, 2 + t:3 + t]).then_inc(af.step(f"ex{t}"), 1)
                if ph == "fa1":
                    act.wait_ge(*pf.at("x2t", b))
                    copy(xt[:, :, :], two(F[0]), af, "x2t")
                if ph == "fa2":
                    act.wait_ge(*pf.at("rl", b))
                    a.activation(lg0[:, :, :], two(F[1])[:, :, 0:E0], ACT.Tanh, scale=0.5)\
                        .then_inc(af.step("lg0"), 1)
                if ph == "fa3":
                    act.wait_ge(*pf.at("z_t", b))
                    copy(z_t[:, :, :], two(F[2])[0:LR, :, :], af, "z_t")
                if ph in FFN_G:
                    m = FFN_G.index(ph)
                    act.wait_ge(*pf.at(f"gu{m}", b))
                    if m >= 2:
                        act.wait_ge(*df.at(f"hid{m - 2}", b))
                    a.activation(tf[:, m % 2, :], F[3 * (m % 2)][:, 0:S], ACT.Tanh, scale=0.5)\
                        .then_inc(af.step(f"tf{m}"), 1)
                if ph == "fd2":
                    act.wait_ge(*pf.at("zd_t", b))
                    copy(zd_t, F[0][0:LR, 0:S], af, "zd_t")
                if ph == "m1":
                    act.wait_ge(*df.at("x3", b))
                    for t in range(TT):
                        a.activation(sqj[:, t, :], xa[:, t, :], ACT.Square, accum_out=small[:, 4 + t:5 + t])\
                            .then_inc(af.step(f"sq{t}"), 1)
                if ph == "m2":
                    act.wait_ge(*pf.at("xnt", b))
                    for k in range(KT):
                        copy(xt[:, k, :], two(F[0])[:, k, :], af, f"xnt{k}", scale=vec[:, V_WN + k:V_WN + k + 1])
                if ph == "m3":
                    for i in range(2):
                        act.wait_ge(*pf.at(f"xs{i}", b))
                        copy(xc[:, 2 * i:2 * i + 2, NCONV - 1:], two(F[1 + i]), af, f"xc{i}")
                if ph in ("m4", "m5"):
                    i = ("m4", "m5").index(ph)
                    act.wait_ge(*df.at(f"conv{i}", b))
                    half = slice(512 * i, 512 * i + 512)
                    a.activation(th_u[:, half], acc[:, half], ACT.Tanh, scale=0.5).then_inc(af.step(f"th_u{i}"), 1)
                if ph == "m4":
                    for i in range(2):
                        act.wait_ge(*pf.at(f"res{i}", b))
                        a.activation(th_c[:, 512 * i:512 * i + 512], F[3 - 3 * i][:, :], ACT.Tanh, scale=0.5)\
                            .then_inc(af.step(f"th_r{i}"), 1)
                if ph == "d1":
                    act.wait_ge(*pf.at("dtr", b))
                    copy(dtr[:, :], F[1][:, 0:S], af, "dtr", scale=0.5)
                if ph == "d2":
                    for d in range(DT):
                        bank = F[3 - 3 * (d // 2)]
                        act.wait_ge(*pf.at(f"dl{d // 2}", b))
                        z = two(bank)[:, d % 2, :]
                        bias = vec[:, V_BDT + d:V_BDT + d + 1]
                        a.activation(e1[:, S * d:S * d + S], z, ACT.Abs, bias=bias).then_inc(af.step(f"az{d}"), 1)
                        a.activation(t_rz[:, S * d:S * d + S], z, ACT.Relu, bias=bias).then_inc(af.step(f"rz{d}"), 1)
                    act.wait_ge(*pf.at("bct", b))
                    copy(bct[:, :], F[2][0:32, 0:S], af, "bct", scale=vec[0:32, V_BCS:V_BCS + 1])
                    act.wait_ge(*af.last(b))
                    a.activation(e1, e1, ACT.Exp, scale=-1.0).then_inc(af.step("e1"), 1)
                if ph == "d3":
                    act.wait_ge(*df.at("w1", b))
                    a.activation(t_ln, t_w, ACT.Ln).then_inc(af.step("ln"), 1)
                if ph == "d4":
                    act.wait_ge(*df.at("delta", b))
                    for i in range(4):
                        replicate(b, 0, i)
                    scan_decay(b, 0)
                if ph in STEPS:
                    n = STEPS.index(ph)
                    ng, d = divmod(n, DT)
                    if n + 1 < NSTEP:
                        scan_decay(b, n + 1)
                    if ng + 1 < NS // NG:
                        replicate(b, ng + 1, d)

            def scan_decay(b, n):
                ng, d = divmod(n, DT)
                if n >= 2:
                    act.wait_ge(*df.at(f"scan{n - 2}", b))
                for s in range(NG):
                    j = d * NS + ng * NG + s
                    ins_ = a.activation(dA[:, n % 2, s, 1:S], delta[:, d, 1:S], ACT.Exp, scale=a_neg[:, j:j + 1])
                ins_.then_inc(af.step(f"dA{n}"), 1)

            def replicate(b, ng, i):
                act.wait_ge(*pf.at(f"rep{ng}_{i}", b))
                if ng >= 2:
                    act.wait_ge(*df.at(f"hc{4 * (ng - 1) - 1}", b))
                copy(rep[:, ng % 2, i // 2, 512 * (i % 2):512 * (i % 2) + 512], F[i % 2][:, :], af, f"rep{ng}_{i}")

            def back(b, ph):
                if ph == "bq1":
                    for i in (0, 2):
                        act.wait_ge(*pb.at(f"kt{i}", b))
                        copy(k_t[:, 2 * i:2 * i + 2, :, :].rearrange("p g v t -> p (g v t)"), halfword(K[i]), ab,
                             f"kt{i}")
                if ph == "bq2":
                    act.wait_ge(*pb.at("kt3", b))
                    act.wait_ge(*df.at("x4", b))
                    xf = x4[:, :, :].rearrange("p t (h d) -> p (t h) d", d=HD1)
                    qf = xq[:, :, :].rearrange("p t (h d) -> p (t h) d", d=HD1)
                    copy(q_sl[:, :, 0:8], xf, ab, "qh")
                    act.wait_ge(*db.at("qr", b))
                    copy(q_sl[:, :, 16:24], qf, ab, "qm")
                    act.wait_ge(*db.at("qr2", b))
                    copy(q_sl[:, :, 40:48], qf, ab, "ql")
                if ph == "bq3":
                    for i in (0, 2):
                        act.wait_ge(*pb.at(f"qt{i}", b))
                        copy(q_t[:, 4 * i:4 * i + 4, :].rearrange("p h t -> p (h t)"), halfword(K[i]), ab, f"qt{i}")
                if ph in BG:
                    gi, half = divmod(BG.index(ph), 2)
                    if gi == 0 and half == 0:
                        act.wait_ge(*pb.at("nm_t", b))
                        copy(nm_t[0:32, :], halfword(K[2])[0:32, 0:S], ab, "nm_t")
                    for j in (2 * half, 2 * half + 1):
                        m = 4 * gi + j
                        act.wait_ge(*pb.at(f"sT{m}", b))
                        if gi >= 1:
                            act.wait_ge(*pb.at(f"av{gi - 1}" if half else f"avh{gi - 1}", b))
                        a.activation(probs[:, m % 4, :], K[m % 2][:, :], ACT.Exp).then_inc(ab.step(f"p{m}"), 1)
                if ph == "br1":
                    act.wait_ge(*pb.at("x5t", b))
                    copy(x5t[:, :, :], two(K[0]), ab, "x5t")
                if ph == "br2":
                    act.wait_ge(*pb.at("lg", b))
                    copy(lg1[:, :, :], two(K[1])[:, :, 0:E1 + 1], ab, "lg1")
                    act.wait_ge(*db.at("nm1", b))
                    for t in range(TT):
                        a.activation(pr1[:, t, 0:E1], lg1[:, t, 0:E1], ACT.Exp, bias=smb[:, t:t + 1],
                                     accum_out=smb[:, 2 + t:3 + t]).then_inc(ab.step(f"pr{t}"), 1)
                    a.activation(smb[:, 4:6], lg1[:, :, E1:E1 + 1].rearrange("p t o -> p (t o)"), ACT.Tanh, scale=0.5)\
                        .then_inc(ab.step("tsg"), 1)
                if ph == "br3":
                    act.wait_ge(*pb.at("c_t", b))
                    copy(c_t[0:96, :], halfword(K[2])[0:96, 0:S], ab, "c_t")
                if ph in BE:
                    m = BE.index(ph)
                    p = m // 2
                    act.wait_ge(*pb.at(f"gu{m}", b))
                    if m >= 2:
                        act.wait_ge(*db.at(f"gu{m - 2}", b))
                    a.activation(thg[:, m % 2, :], K[m % 2][:, 0:S], ACT.Tanh, scale=0.5)\
                        .then_inc(ab.step(f"th{m}"), 1)
                    if m % 2 == 0:
                        act.wait_ge(*pb.at(f"cr{p}", b))
                        if p >= 2:
                            act.wait_ge(*gb.at(f"hid{2 * p - 3}", b))
                        copy(crs[:, p % 2, :, :], two(K[2]), ab, f"cr{p}")

            run(act, front, back, [af], [ab], ORDER)

        @block.tensor
        def _(pe):
            t_ = nc.tensor

            def mm(dst, lhsT, rhs, start, stop):
                return t_.matmul(dst, lhsT, rhs, start=start, stop=stop, skip_group_check=True)

            def turn(bank, src, steps_, name):
                for k in range(KT):
                    for t in range(TT):
                        last = t_.transpose(bank[:, k * S + t * P:k * S + t * P + P], src[:, t, k * P:k * P + P],
                                            ident[:, :])
                last.then_inc(steps_.step(name), 1)

            def project(bank, w, cols, src, steps_, name):
                for i, c in enumerate(cols):
                    for k in range(KT):
                        last = mm(bank[:, i * S:i * S + S], w[:, k, c:c + P], src[:, k, :], k == 0, k == KT - 1)
                last.then_inc(steps_.step(name), 1)

            def linear_av(b, q):
                f, par = q // 2, q % 2
                for s in range(TT):
                    for j in range(4):
                        r = (4 * q + j) % A_RING
                        w = att[:, r, 0:S] if s == 0 else att[:, r, S:S + P]
                        last = t_.matmul(F[3][32 * j:32 * j + 32, f * S + s * P:f * S + S],
                                         vz[:, s, 8 * f + 2 * j + par, :], w,
                                         start=(par == 0 and s == 0), stop=(par == 1 and s == 1),
                                         skip_group_check=True)
                last.then_inc(pf.step(f"av{q}"), 1)

            def replicate(b, ng, i):
                if ng == 0:
                    if i < 2:
                        pe.wait_ge(*df.at("bcp", b))
                        pe.wait_ge(*af.at("rz3", b))
                    else:
                        pe.wait_ge(*af.at(f"rep0_{i - 2}", b))
                else:
                    pe.wait_ge(*af.at(f"rep{ng}_{i - 2}" if i >= 2 else f"rep{ng - 1}_{i + 2}", b))
                for k in range(2):
                    j = (i // 2) * NS + ng * NG + 2 * (i % 2) + k
                    last = mm(F[i % 2][:, k * S:k * S + S], pick[:, j:j + 1].to_broadcast([P, P]), bcp[:, :],
                              True, True)
                last.then_inc(pf.step(f"rep{ng}_{i}"), 1)

            def gate_up(m):
                for u, w in enumerate((wgate, wup)):
                    for k in range(KT):
                        mm(F[3 * (m % 2)][:, u * S:u * S + S], w[:, k, m * P:m * P + P], xt[:, k, :],
                           k == 0 and u == 0, False)

            def down0(m):
                for t in range(TT):
                    last = mm(F[1 + t][:, 0:FDN], hid0[:, m, t * P:t * P + P], wdown[:, m, :],
                              m == 0, m == MT0 - 1)
                return last

            def sum_states(b, n):
                ng, d = divmod(n, DT)
                pe.wait_ge(*df.at(f"hc{n}", b))
                terms = NG // 2 if in_pairs(b, n) else NG
                for s in range(terms):
                    last = mm(F[2 + d // 2][:, (d % 2) * S:(d % 2) * S + S], ident[:, :],
                              hb[:, n % 4, s * S:s * S + S], ng == 0 and s == 0 and d % 2 == 0,
                              ng == NS // NG - 1 and s == terms - 1)
                last.then_inc(pf.step(f"y{n}"), 1)

            def scan_out(b, i):
                pe.wait_ge(*df.at(f"yz{i}", b))
                for d in (2 * i, 2 * i + 1):
                    for t in range(TT):
                        last = mm(F[0][:, t * D:t * D + D], yz[:, d, t * P:t * P + P], wmo[:, d, :],
                                  d == 0 and t == 0, d == DT - 1)
                return last

            def front(b, ph):
                if ph == "qkv":
                    if not later(b):
                        pe.wait_ge(consts_in, 64)
                    else:
                        pe.wait_ge(*df.at("yz1", b - 1))
                    pe.wait_ge(x_in, b * 48 + 48)
                    pe.wait_ge(l0_in, b * 16 + 16)
                    project(F[1], wqkvu, (0, P), x_t, pf, "q")
                    project(F[2], wqkvu, (D, D + P), x_t, pf, "k")
                    project(F[3], wqkvu, (3 * D, 3 * D + P), x_t, pf, "u")
                    if later(b):
                        pe.wait_ge(*df.end(b - 1))
                    for t in range(TT):
                        for k in range(KT):
                            last = mm(F[0][:, t * D:t * D + D], x_t[:, k, t * P:t * P + P],
                                      wqkvu[:, k, 2 * D:3 * D], k == 0, k == KT - 1)
                    last.then_inc(pf.step("v"), 1)
                if ph in PAIRS:
                    i = PAIRS.index(ph)
                    for n in (2 * i, 2 * i + 1):
                        f, v = divmod(head(n), 8)
                        if n == 0:
                            pe.wait_ge(*df.at("qs", b))
                        if n < 3:
                            pe.wait_ge(*[af.at("vz1", b), df.at("qs", b), df.at("ks", b)][n])
                        else:
                            pe.wait_ge(*(af.at(f"c{n - 3}", b) if n % 2 == 0 else df.at(f"a{n - 3}", b)))
                        pe.wait_ge(*df.at(f"kz{v}", b))
                        bank = F[n % 3]
                        qf = qs.rearrange("p (f t) -> p f t", f=KT)
                        mm(bank[:, 0:S], kz[:, f, v, 0:P], qf[:, f, :], True, True)
                        mm(bank[:, S:S + P], kz[:, f, v, P:S], qf[:, f, P:S], True, True)\
                            .then_inc(pf.step(f"s{n}"), 1)
                    if i == 0:
                        pe.wait_ge(*af.at("us", b))
                    if i % 2 == 0 and i:
                        q = i // 2
                        pe.wait_ge(*df.at(f"a{4 * q - 2}", b))
                        pe.wait_ge(*gf.at(f"a{4 * q - 1}", b))
                        linear_av(b, q - 1)
                if ph == "oa":
                    if not later(b):
                        pe.wait_ge(init_v, N_INIT_V)
                        pe.wait_ge(init, N_INIT)
                    pe.wait_ge(*df.at("a14", b))
                    pe.wait_ge(*gf.at("a15", b))
                    linear_av(b, 3)
                    for t in range(TT):
                        last = mm(F[2][:, t * CD:t * CD + CD], ctx_t[:, t * P:t * P + P], wk[:, :], True, True)
                    last.then_inc(pf.step("kv_tok"), 1)
                    mm(F[1][0:CD, 0:S], wk[:, :], ctx_t[:, :], True, True).then_inc(pf.step("kv_t"), 1)
                if ph == "ob":
                    pe.wait_ge(*df.at("kv", b))
                    pe.wait_ge(*af.at("osq", b))
                    o2 = osq.rearrange("p (f t) -> p f t", f=KT)
                    for t in range(TT):
                        for f in range(KT):
                            last = mm(F[2][:, t:t + 1], o2[:, f, t * P:t * P + P], ones[:, :], f == 0, f == KT - 1)
                    last.then_inc(pf.step("ssq"), 1)
                    pe.wait_ge(*df.at("uo", b))
                    u_ = uo.rearrange("p (f t) -> p f t", f=KT)
                    for t in range(TT):
                        for f in range(KT):
                            last = mm(F[0][:, t * D:t * D + D], u_[:, f, t * P:t * P + P], wo0[:, f, :],
                                      f == 0, f == KT - 1)
                    last.then_inc(pf.step("wo"), 1)
                if ph == "xa":
                    pe.wait_ge(*df.at("x1", b))
                    turn(F[0], xa, pf, "x1t")
                if ph == "xb":
                    pe.wait_ge(*af.at("x1t", b))
                    for t in range(TT):
                        last = mm(F[3][0:CD, 0:S], kv[:, t, :], xt[:, t, :], t == 0, t == TT - 1)
                    last.then_inc(pf.step("o_t"), 1)
                if ph == "xc":
                    pe.wait_ge(*af.at("o_t", b))
                    for t in range(TT):
                        last = mm(F[1][:, t * S:t * S + S], o_t[:, t * P:t * P + P], kv_t[:, :], True, True)
                    last.then_inc(pf.step("sim"), 1)
                if ph == "fa1":
                    if not later(b):
                        pe.wait_ge(weights_in, 48)
                    pe.wait_ge(f_in, b * 16 + 16)
                    pe.wait_ge(*df.at("x2", b))
                    turn(F[0], xb, pf, "x2t")
                if ph == "fa2":
                    pe.wait_ge(*af.at("x2t", b))
                    for t in range(TT):
                        for k in range(KT):
                            last = mm(two(F[1])[:, t, 0:FA], xt[:, k, t * P:t * P + P], wrouter0[:, k, :],
                                      k == 0, k == KT - 1)
                    last.then_inc(pf.step("rl"), 1)
                    gate_up(0)
                    gate_up(1)
                if ph == "fa3":
                    pe.wait_ge(*df.at("zz", b))
                    for u in range(2):
                        for t in range(TT):
                            last = t_.transpose(F[2][0:LR, u * S + t * P:u * S + t * P + P],
                                                zz[:, t, u * LR:u * LR + LR], ident[:, :])
                    last.then_inc(pf.step("z_t"), 1)
                if ph in FFN_G:
                    m = FFN_G.index(ph)
                    if m == 0:
                        pe.wait_ge(*af.at("z_t", b))
                    for u, lb in enumerate((bgate, bup)):
                        last = mm(F[3 * (m % 2)][:, u * S:u * S + S], lb[:, m * P:m * P + P], z_t[:, u, :],
                                  False, u == 1)
                    last.then_inc(pf.step(f"gu{m}"), 1)
                    if m >= 1:
                        pe.wait_ge(*df.at(f"hid{m - 1}", b))
                        if m + 1 < MT0:
                            gate_up(m + 1)
                        down0(m - 1)
                if ph == "fd1":
                    pe.wait_ge(*df.at(f"hid{MT0 - 1}", b))
                    down0(MT0 - 1).then_inc(pf.step("down"), 1)
                if ph == "fd2":
                    pe.wait_ge(*df.at("zd1", b))
                    for t in range(TT):
                        last = t_.transpose(F[0][0:LR, t * P:t * P + P], zd[:, t, :], ident[:, :])
                    last.then_inc(pf.step("zd_t"), 1)
                if ph == "fd3":
                    pe.wait_ge(*af.at("zd_t", b))
                    for t in range(TT):
                        last = mm(F[1 + t][:, 0:D], zd_t[:, t * P:t * P + P], bdown, False, True)
                    last.then_inc(pf.step("down2"), 1)
                if ph == "m2":
                    pe.wait_ge(*df.at("xn", b))
                    turn(F[0], xp, pf, "xnt")
                if ph == "m3":
                    pe.wait_ge(*af.at("xnt1", b))
                    project(F[1], win, (0, P), xt, pf, "xs0")
                    project(F[2], win, (2 * P, 3 * P), xt, pf, "xs1")
                if ph == "m4":
                    project(F[3], win, (4 * P, 5 * P), xt, pf, "res0")
                    project(F[0], win, (6 * P, 7 * P), xt, pf, "res1")
                if ph == "d1":
                    for d in range(DT):
                        if d % 2 == 0:
                            pe.wait_ge(*df.at(f"u2_{d // 2}", b))
                        last = mm(F[1][:, 0:S], wxp[:, d, 0:DTR], u2[:, d, :], d == 0, d == DT - 1)
                    last.then_inc(pf.step("dtr"), 1)
                if ph == "d2":
                    pe.wait_ge(*af.at("dtr", b))
                    for i in range(2):
                        for d in range(2):
                            c = (2 * i + d) * P
                            last = mm(F[3 - 3 * i][:, d * S:d * S + S], wdt[:, c:c + P], dtr[:, :], True, True)
                        last.then_inc(pf.step(f"dl{i}"), 1)
                    for d in range(DT):
                        last = mm(F[2][0:32, 0:S], wxp[:, d, DTR:DTR + 2 * NS], u2[:, d, :], d == 0, d == DT - 1)
                    last.then_inc(pf.step("bct"), 1)
                if ph == "d4":
                    for i in range(4):
                        replicate(b, 0, i)
                if ph in STEPS:
                    n = STEPS.index(ph)
                    ng, d = divmod(n, DT)
                    if ng + 1 < NS // NG:
                        replicate(b, ng + 1, d)
                    if n >= 1:
                        sum_states(b, n - 1)
                if ph == "u1":
                    sum_states(b, NSTEP - 1)
                    scan_out(b, 0)
                if ph == "u2":
                    if not later(b):
                        pe.wait_ge(expand_filled, 10)
                    last = scan_out(b, 1)
                    last.then_inc(pf.step("mo"), 1)

            def attend(b, g, t):
                if t == 0 and g >= 2:
                    pe.wait_ge(*db.at(f"ao{g - 2}", b))
                for j in range(4):
                    i, v = divmod(j, 2)
                    m = 4 * g + 2 * t + v
                    pe.wait_ge(*ab.at(f"p{m}", b))
                    last = t_.matmul(K[2 + g % 2][32 * j:32 * j + 32, 0:S], v32[:, t, g, :],
                                     probs[:, m % 4, i * S:i * S + S], start=(t == 0), stop=(t == TT - 1),
                                     skip_group_check=True)
                last.then_inc(pb.step(f"av{g}" if t == TT - 1 else f"avh{g}"), 1)

            def expert_down(b, m):
                pe.wait_ge(*gb.at(f"hid{m}", b))
                for t in range(TT):
                    last = mm(K[3][:, t * D:t * D + D], hid1[:, m % 3, t * P:t * P + P],
                              mw[:, m % MW_RING, 2 * D:3 * D],
                              m == 0 and t == 0, m == MT1 - 1)
                last.then_inc(pb.step(f"down{m}"), 1)

            def back(b, ph):
                if ph in ("bq1", "bq3"):
                    if ph == "bq1":
                        pe.wait_ge(*db.end(b - 1))
                        pe.wait_ge(*gf.at("k_split", b))
                    else:
                        pe.wait_ge(*db.at("qsl", b))
                        pe.wait_ge(*ab.at("ql", b))
                    name, src = ("kt", k_tr) if ph == "bq1" else ("qt", q_tr)
                    for i in range(4):
                        hw = halfword(K[i])
                        for h in range(4):
                            for t in range(TT):
                                last = t_.transpose(hw[:, h * S + t * P:h * S + t * P + P],
                                                    src[:, t, 4 * i + h, :], ident_bf[:, :])
                        last.then_inc(pb.step(f"{name}{i}"), 1)
                if ph in BMAX:
                    for c in range(2):
                        n = 2 * BMAX.index(ph) + c
                        s, hp = divmod(n, HQ // 2)
                        if n < 4:
                            if n == 0:
                                pe.wait_ge(*ab.at("qt2", b))
                                pe.wait_ge(*db.at("qt3", b))
                        else:
                            pe.wait_ge(*db.at(f"mx{n - 4}", b))
                        mm(K[n % 4][:, :], q_t[:, hp, s * P:s * P + P],
                           k_t[:, hp // 2, :, :].rearrange("p v t -> p (v t)"), True, True)\
                            .then_inc(pb.step(f"ms{n}"), 1)
                if ph in BG:
                    g, t = divmod(BG.index(ph), 2)
                    if g == 0 and t == 0:
                        pe.wait_ge(*db.at("nmb", b))
                        hw = halfword(K[2])
                        for i in range(TT):
                            last = t_.transpose(hw[0:32, i * P:i * P + P], nmb[:, i, :], ident_bf[:, :])
                        last.then_inc(pb.step("nm_t"), 1)
                        pe.wait_ge(*ab.at("nm_t", b))
                    for v in range(2):
                        m = 4 * g + 2 * t + v
                        if m >= 2:
                            pe.wait_ge(*ab.at(f"p{m - 2}", b))
                        mm(K[m % 2][:, :], k_t[:, g, v, t * P:t * P + P],
                           q_t[:, 2 * g:2 * g + 2, :].rearrange("p h t -> p (h t)"), True, False)
                        for i in range(2):
                            h = 4 * g + 2 * i + v
                            last = mm(K[m % 2][:, i * S:i * S + S], pick[:, h:h + 1].to_broadcast([P, P]),
                                      nm_t[:, :], False, i == 1)
                        last.then_inc(pb.step(f"sT{m}"), 1)
                    if t == 1:
                        attend(b, g, 0)
                    elif g >= 1:
                        attend(b, g - 1, 1)
                if ph == "ba1":
                    attend(b, HKV - 1, 1)
                if ph == "ba2":
                    for i in range(4):
                        s, half = divmod(i, 2)
                        if i == 0:
                            pe.wait_ge(*db.at("ao7", b))
                        for g in range(4):
                            last = t_.transpose(K[i][:, g * P:g * P + P], ao[:, 4 * half + g, s * P:s * P + P],
                                                ident[:, :])
                        last.then_inc(pb.step(f"ot{i}"), 1)
                if ph == "br1":
                    pe.wait_ge(*db.at("x5", b))
                    turn(K[0], x5, pb, "x5t")
                if ph == "br2":
                    pe.wait_ge(*ab.at("x5t", b))
                    for t in range(TT):
                        for k in range(KT):
                            last = mm(two(K[1])[:, t, 0:E1 + 1], x5t[:, k, t * P:t * P + P], wr1[:, k, :],
                                      k == 0, k == KT - 1)
                    last.then_inc(pb.step("lg"), 1)
                if ph == "br3":
                    pe.wait_ge(*db.at("cp", b))
                    hw = halfword(K[2])
                    for t in range(TT):
                        last = t_.transpose(hw[0:96, t * P:t * P + P], cp[:, t, :], ident_bf[:, :])
                    last.then_inc(pb.step("c_t"), 1)
                if ph in BE:
                    m = BE.index(ph)
                    p, slot = m // 2, m % MW_RING
                    pe.wait_ge(mw_in[slot], b * (len(range(slot, MT1, MW_RING)) * 16) + (m // MW_RING) * 16 + 16)
                    if m >= 2:
                        pe.wait_ge(*db.at(f"gu{m - 2}", b))
                    for u in range(2):
                        for k in range(KT):
                            c = u * D + k * P
                            last = mm(K[m % 2][:, u * S:u * S + S], mw[:, slot, c:c + P], x5t[:, k, :],
                                      k == 0, k == KT - 1)
                    last.then_inc(pb.step(f"gu{m}"), 1)
                    if m % 2 == 0:
                        pe.wait_ge(*ab.at("c_t" if p == 0 else f"cr{p - 1}", b))
                        for i in range(2):
                            c = (m + i) * P
                            last = mm(K[2][:, i * S:i * S + S], expand[:, c:c + P], c_t[:, :], True, True)
                        last.then_inc(pb.step(f"cr{p}"), 1)
                    if m >= 2:
                        expert_down(b, m - 2)
                if ph == "bout":
                    expert_down(b, MT1 - 2)
                    expert_down(b, MT1 - 1)

            run(pe, front, back, [pf], [pb], ORDER_PE)

        @block.vector
        def _(dve):
            v = nc.vector
            dve.wait_ge(consts_in, 64)
            v.tensor_copy(ident[:, :], arena[:, C_IDENT:C_IDENT + P]).then_inc(init_v, 1)
            v.tensor_copy(ident_bf[:, :], arena[:, C_IDENT:C_IDENT + P]).then_inc(init_v, 1)
            v.tensor_scalar(headmask[:, :], arena[:, C_HEADMASK:C_HEADMASK + 8], 0.25, None, ALU.mult)\
                .then_inc(init_v, 1)
            v.tensor_scalar(rows[:, R_SLOPE:R_END], rows[:, R_SLOPE:R_END], -1.0, None, ALU.mult).then_inc(init_v, 1)
            v.tensor_copy(pick[:, :], arena[:, C_PARTID:C_PARTID + 32])
            v.tensor_scalar(d_half[:, :], vec[:, V_D:V_D + DT], 0.5, None, ALU.mult).then_inc(init_v, 1)
            dve.wait_ge(init_a, N_INIT_A)
            v.tensor_scalar(a_neg[:, :], a_neg[:, :], -1.0, None, ALU.mult)
            v.tensor_tensor(decay[:, :, :], decay[:, :, :],
                            arena[:, C_CAUSAL:C_CAUSAL + S].unsqueeze(1).to_broadcast([P, H0, S]), ALU.mult)\
                .then_inc(init_v, 1)
            dve.wait_ge(init_v, N_INIT_V)

            def own(steps_, b):
                dve.wait_ge(*steps_.last(b))

            def settle():
                v.memset(idle_v[:, :], 0.0)

            def layernorm(b, src, dst, steps_, rsq, name, st, mvt, vet, rst):
                own(steps_, b)
                for t in range(TT):
                    v.bn_stats(st[:, t, :], src[:, t, :]).then_inc(steps_.step(), 1)
                own(steps_, b)
                settle()
                for t in range(TT):
                    v.bn_aggr(mvt[:, t, :], st[:, t, :]).then_inc(steps_.step(), 1)
                own(steps_, b)
                v.tensor_scalar(vet[:, :], mvt[:, :, 1:2].rearrange("p t o -> p (t o)"), 1e-5, None, ALU.add)\
                    .then_inc(steps_.step(f"ve_{name}"), 1)
                dve.wait_ge(*rsq.at(f"rs_{name}", b))
                for t in range(TT):
                    v.tensor_scalar(dst[:, t, :], src[:, t, :], mvt[:, t, 0:1], rst[:, t:t + 1],
                                    ALU.subtract, ALU.mult).then_inc(steps_.step(), 1)

            def ln_front(b, dst, name, mark):
                layernorm(b, xp, dst, df, gf, name, st6, mv, ve, rs)
                df.number[mark] = df.count

            def top(bi, v8, tr, rp, k, width, steps_, b):
                settle()
                for t in range(TT):
                    v.max(v8[:, t, :], bi[:, t, 0:width]).then_inc(steps_.step(), 1)
                own(steps_, b)
                v.tensor_copy(tr[:, :, 0:k], v8[:, :, 0:k]).then_inc(steps_.step(), 1)
                own(steps_, b)
                settle()
                for t in range(TT):
                    v.match_replace(rp[:, t, :], tr[:, t, :], bi[:, t, :], 2 * NEG).then_inc(steps_.step(), 1)
                own(steps_, b)

            def front(b, ph):
                if ph == "qkv":
                    for th, bank, dst, name in ((th_a, F[1], qs, "q"), (th_b, F[2], ks, "k")):
                        dve.wait_ge(*af.at(f"th_{name}", b))
                        v.scalar_tensor_tensor(dst, th, 1.0, bank[:, :], ALU.add, ALU.mult)\
                            .then_inc(df.step(f"{name}s"), 1)
                    own(df, b)
                    if later(b):
                        dve.wait_ge(*pf.at("mo", b - 1))
                    for c in (0, 2, 4, 6, 1, 3, 5, 7):
                        v.tensor_scalar(kz[:, :, c, :], ks.rearrange("p (f t) -> p f t", f=KT),
                                        headmask[:, c:c + 1], None, ALU.mult).then_inc(df.step(f"kz{c}"), 1)
                if ph in PAIRS:
                    n = 2 * PAIRS.index(ph)
                    h = head(n)
                    if n >= A_RING:
                        dve.wait_ge(*pf.at(f"av{(n - A_RING) // 4}", b))
                    dve.wait_ge(*pf.at(f"s{n}", b))
                    r = n % A_RING
                    v.tensor_tensor(att[:, r, 0:S], F[n % 3][:, 0:S], decay[:, h, :], ALU.mult)\
                        .then_inc(df.step(), 1)
                    v.tensor_tensor(att[:, r, S:S + P], F[n % 3][:, S:S + P], decay[:, h, 0:P], ALU.mult)\
                        .then_inc(df.step(f"a{n}"), 1)
                if ph == "oa":
                    if not later(b):
                        dve.wait_ge(init, N_INIT)
                    dve.wait_ge(*af.at("osq", b))
                    v.tensor_tensor(uo, F[3][:, :], us, ALU.mult).then_inc(df.step("uo"), 1)
                    dve.wait_ge(*pf.at("kv_tok", b))
                    v.tensor_tensor(kv[:, :, :], F[2][:, 0:TT * CD].rearrange("p (t c) -> p t c", t=TT),
                                    rows[:, R_BK:R_BK + CD].unsqueeze(1).to_broadcast([P, TT, CD]), ALU.add)\
                        .then_inc(df.step("kv"), 1)
                if ph == "ob":
                    dve.wait_ge(*pf.at("ssq", b))
                    v.tensor_scalar(ve[:, :], F[2][:, 0:TT], 1.0 / D, 1e-6, ALU.mult, ALU.add)\
                        .then_inc(df.step("ve_o"), 1)
                    dve.wait_ge(*gf.at("rs_o", b))
                    dve.wait_ge(*pf.at("wo", b))
                    for t in range(TT):
                        v.scalar_tensor_tensor(xp[:, t, :], two(F[0])[:, t, :], rs[:, t:t + 1], x_tok[:, t, :],
                                               ALU.mult, ALU.add).then_inc(df.step("x_tok_read"), 1)
                    ln_front(b, xa, "ln1", "x1")
                if ph == "xc":
                    dve.wait_ge(*pf.at("sim", b))
                    for t in range(TT):
                        v.bn_stats(st6[:, t, :], two(F[1])[:, t, :]).then_inc(df.step(), 1)
                    own(df, b)
                    settle()
                    for t in range(TT):
                        v.bn_aggr(mv[:, t, :], st6[:, t, :]).then_inc(df.step(), 1)
                    own(df, b)
                    v.tensor_scalar(ve[:, :], mv[:, :, 1:2].rearrange("p t o -> p (t o)"), 1.0 / D, 1e-6,
                                    ALU.mult, ALU.add).then_inc(df.step("ve_sim"), 1)
                    for t in range(TT):
                        v.scalar_tensor_tensor(en[:, t, :], two(F[1])[:, t, :], mv[:, t, 0:1],
                                               rows[:, R_GAMMA:R_GAMMA + S], ALU.subtract, ALU.mult)\
                            .then_inc(df.step(), 1)
                    dve.wait_ge(*gf.at("rs_sim", b))
                    v.tensor_scalar(small[:, 8:10], rs[:, :], float(D) ** -0.5, None, ALU.mult).then_inc(df.step(), 1)
                    own(df, b)
                    for t in range(TT):
                        v.scalar_tensor_tensor(en[:, t, :], en[:, t, :], small[:, 8 + t:9 + t],
                                               rows[:, R_BETA:R_BETA + S], ALU.mult, ALU.add).then_inc(df.step(), 1)
                    own(df, b)
                    v.tensor_reduce(small[:, 0:2], en, AX_X, ALU.max, negate=True).then_inc(df.step("nmx"), 1)
                if ph == "xd":
                    dve.wait_ge(*af.at("ex1", b))
                    v.reciprocal(small[:, 10:12], small[:, 2:4]).then_inc(df.step(), 1)
                    own(df, b)
                    for t in range(TT):
                        v.scalar_tensor_tensor(xp[:, t, :], ee[:, t, :], small[:, 10 + t:11 + t], xa[:, t, :],
                                               ALU.mult, ALU.add).then_inc(df.step(), 1)
                    ln_front(b, xb, "ln2", "x2")
                if ph == "fa2":
                    dve.wait_ge(*af.at("lg0", b))
                    v.tensor_scalar(sc0[:, :, :], lg0[:, :, :], 0.5, 0.5, ALU.mult, ALU.add).then_inc(df.step(), 1)
                    own(df, b)
                    v.tensor_tensor(bi0[:, :, 0:E0], sc0[:, :, :],
                                    rows[:, R_EB:R_EB + E0].unsqueeze(1).to_broadcast([P, TT, E0]), ALU.add)\
                        .then_inc(df.step(), 1)
                    own(df, b)
                    top(bi0, v80, tr0, rp0, 2, E0, df, b)
                    v.scalar_tensor_tensor(sc0[:, :, :], rp0[:, :, 0:E0], 2 * NEG, sc0[:, :, :], ALU.is_equal,
                                           ALU.mult).then_inc(df.step(), 1)
                    own(df, b)
                    v.tensor_reduce(small[:, 0:2], sc0[:, :, :], AX_X, ALU.add).then_inc(df.step(), 1)
                    own(df, b)
                    v.tensor_scalar(small[:, 2:4], small[:, 0:2], 1e-8, None, ALU.add).then_inc(df.step(), 1)
                    own(df, b)
                    v.reciprocal(small[:, 0:2], small[:, 2:4]).then_inc(df.step(), 1)
                    own(df, b)
                    for t in range(TT):
                        v.tensor_scalar(w9[:, t, 0:E0], sc0[:, t, :], small[:, t:t + 1], 1.0 / RANK,
                                        ALU.mult, ALU.mult).then_inc(df.step(), 1)
                    own(df, b)
                    for t in range(TT):
                        v.tensor_tensor(zz[:, t, :].rearrange("p (u e r) -> p u e r", u=2, e=E0S),
                                        two(F[1])[:, t, E0:FA].rearrange("p (u e r) -> p u e r", u=2, e=E0S),
                                        w9[:, t, :].unsqueeze(1).unsqueeze(3).to_broadcast([P, 2, E0S, RANK]),
                                        ALU.mult).then_inc(df.step("zz"), 1)
                if ph in FFN_G:
                    m = FFN_G.index(ph)
                    bank = F[3 * (m % 2)]
                    dve.wait_ge(*af.at(f"tf{m}", b))
                    v.scalar_tensor_tensor(ta[:, m % 2, :], tf[:, m % 2, :], 1.0, bank[:, 0:S], ALU.add, ALU.mult)\
                        .then_inc(df.step(), 1)
                    own(df, b)
                    v.scalar_tensor_tensor(hid0[:, m, :], ta[:, m % 2, :], 0.5, bank[:, S:2 * S], ALU.mult, ALU.mult)\
                        .then_inc(df.step(f"hid{m}"), 1)
                if ph == "fd1":
                    dve.wait_ge(*pf.at("down", b))
                    for t in range(TT):
                        v.tensor_tensor(zd[:, t, :].rearrange("p (e r) -> p e r", e=E0S),
                                        F[1 + t][:, D:FDN].rearrange("p (e r) -> p e r", e=E0S),
                                        w9[:, t, :].unsqueeze(2).to_broadcast([P, E0S, RANK]), ALU.mult)\
                            .then_inc(df.step(f"zd{t}"), 1)
                if ph == "fd3":
                    dve.wait_ge(*pf.at("down2", b))
                    for t in range(TT):
                        v.tensor_tensor(xp[:, t, :], F[1 + t][:, 0:D], xb[:, t, :], ALU.add).then_inc(df.step(), 1)
                    ln_front(b, xa, "ln3", "x3")
                if ph == "m1":
                    v.memset(xc[:, :, 0:NCONV - 1], 0.0).then_inc(df.step(), 1)
                    dve.wait_ge(*af.at("sq1", b))
                    v.tensor_scalar(ve[:, :], small[:, 4:6], 1.0 / D, 1e-5, ALU.mult, ALU.add)\
                        .then_inc(df.step("ve_rms"), 1)
                    dve.wait_ge(*gf.at("rs_rms", b))
                    for t in range(TT):
                        v.tensor_scalar(xp[:, t, :], xa[:, t, :], rs[:, t:t + 1], None, ALU.mult)\
                            .then_inc(df.step("xn"), 1)
                if ph == "m4":
                    for i in range(2):
                        dve.wait_ge(*af.at(f"xc{i}", b))
                        for k in range(NCONV):
                            if k:
                                own(df, b)
                            for d in (2 * i, 2 * i + 1):
                                c, w = acc[:, S * d:S * d + S], V_CW + 4 * d + k
                                if k == 0:
                                    tap = v.tensor_scalar(c, xc[:, d, 0:S], vec[:, w:w + 1],
                                                          vec[:, V_CB + d:V_CB + d + 1], ALU.mult, ALU.add)
                                else:
                                    tap = v.scalar_tensor_tensor(c, xc[:, d, k:k + S], vec[:, w:w + 1], c,
                                                                 ALU.mult, ALU.add)
                                tap.then_inc(df.step(f"conv{i}"), 1)
                    conv_silu(b, 0)
                    for i in range(2):
                        dve.wait_ge(*af.at(f"th_r{i}", b))
                        v.scalar_tensor_tensor(sres[:, 2 * i:2 * i + 2, :].rearrange("p d t -> p (d t)"),
                                               th_c[:, 512 * i:512 * i + 512], 1.0, F[3 - 3 * i][:, :],
                                               ALU.add, ALU.mult).then_inc(df.step(f"sres{i}"), 1)
                if ph == "m5":
                    conv_silu(b, 1)
                if ph == "d2":
                    dve.wait_ge(*af.at("bct", b))
                    v.tensor_copy(bcp[0:32, :], bct[:, :]).then_inc(df.step(), 1)
                    own(df, b)
                    v.tensor_tensor(bcr[:, :], bct[:, :], bcp[0:32, :], ALU.subtract).then_inc(df.step(), 1)
                    own(df, b)
                    v.tensor_copy(bcm[:, :], bcr[:, :]).then_inc(df.step(), 1)
                    own(df, b)
                    v.tensor_copy(bcp[32:64, :], bcm[:, :]).then_inc(df.step(), 1)
                    v.tensor_tensor(bcr[:, :], bcr[:, :], bcm[:, :], ALU.subtract).then_inc(df.step(), 1)
                    own(df, b)
                    v.tensor_copy(bcp[64:96, :], bcr[:, :]).then_inc(df.step("bcp"), 1)
                    dve.wait_ge(*af.at("e1", b))
                    v.tensor_scalar(t_w, e1, 1.0, None, ALU.add).then_inc(df.step("w1"), 1)
                if ph == "d3":
                    own(df, b)
                    v.scalar_tensor_tensor(e1, t_w, -1.0, e1, ALU.add, ALU.subtract).then_inc(df.step(), 1)
                    own(df, b)
                    v.tensor_tensor(t_rz, t_rz, e1, ALU.subtract).then_inc(df.step(), 1)
                    dve.wait_ge(*af.at("ln", b))
                    own(df, b)
                    dl = delta[:, :, :].rearrange("p d t -> p (d t)")
                    v.tensor_tensor(dl, t_rz, t_ln, ALU.add).then_inc(df.step("delta"), 1)
                    own(df, b)
                    v.memset(dA[:, :, :, 0:1], 0.0).then_inc(df.step("dA0"), 1)
                    own(df, b)
                    v.tensor_tensor(du[:, :, :].rearrange("p d t -> p (d t)"), dl,
                                    u2[:, :, :].rearrange("p d t -> p (d t)"), ALU.mult).then_inc(df.step("du"), 1)
                if ph in STEPS:
                    n = STEPS.index(ph)
                    ng, d = divmod(n, DT)
                    h = hb[:, n % 4, :]
                    dve.wait_ge(*af.at(f"dA{n}", b))
                    dve.wait_ge(*gf.at(f"dbu{n}", b))
                    v.tensor_tensor_scan(h, dA[:, n % 2, :, :].rearrange("p s t -> p (s t)"), h, 0.0,
                                         ALU.mult, ALU.add).then_inc(df.step(f"scan{n}"), 1)
                    dve.wait_ge(*af.at(f"rep{ng}_3", b))
                    own(df, b)
                    hc = v.tensor_tensor(h, h, rep[:, ng % 2, 1, :], ALU.mult)
                    if in_pairs(b, n):
                        hc.then_inc(df.step(), 1)
                        own(df, b)
                        half = NG // 2 * S
                        v.tensor_tensor(h[:, 0:half], h[:, 0:half], h[:, half:], ALU.add)\
                            .then_inc(df.step(f"hc{n}"), 1)
                    else:
                        df.step()
                        hc.then_inc(df.step(f"hc{n}"), 2)
                    if n == NSTEP - 1:
                        gated_output(b, 0)
                if ph == "u1":
                    gated_output(b, 1)
                if ph == "u2":
                    xpf, xaf = (x[:, :, :].rearrange("p t n -> p (t n)") for x in (xp, xa))
                    v.tensor_scalar(xpf, xaf, 2.0, None, ALU.mult).then_inc(df.step(), 1)
                    own(df, b)
                    dve.wait_ge(*pf.at("mo", b))
                    v.scalar_tensor_tensor(xpf, F[0][:, :], 0.5, xpf, ALU.mult, ALU.add).then_inc(df.step(), 1)
                    ln_front(b, x4, "ln4", "x4")

            def conv_silu(b, i):
                dve.wait_ge(*af.at(f"th_u{i}", b))
                half = slice(512 * i, 512 * i + 512)
                v.scalar_tensor_tensor(u2[:, 2 * i:2 * i + 2, :].rearrange("p d t -> p (d t)"), th_u[:, half], 1.0,
                                       acc[:, half], ALU.add, ALU.mult).then_inc(df.step(f"u2_{i}"), 1)

            def gated_output(b, i):
                dve.wait_ge(*pf.at(f"y{NSTEP - DT + 2 * i + 1}", b))
                for d in (2 * i, 2 * i + 1):
                    v.scalar_tensor_tensor(yz[:, d, :], u2[:, d, :], d_half[:, d:d + 1],
                                           two(F[2 + i])[:, d % 2, :], ALU.mult, ALU.add).then_inc(df.step(), 1)
                own(df, b)
                y_ = yz[:, 2 * i:2 * i + 2, :]
                v.tensor_tensor(y_, y_, sres[:, 2 * i:2 * i + 2, :], ALU.mult).then_inc(df.step(f"yz{i}"), 1)

            def back(b, ph):
                x4f, xqf, x5f = (x[:, :, :].rearrange("p t n -> p (t n)") for x in (x4, xq, x5))
                if ph == "bq1":
                    for i in (1, 3):
                        dve.wait_ge(*pb.at(f"kt{i}", b))
                        v.tensor_copy(k_t[:, 2 * i:2 * i + 2, :, :].rearrange("p g v t -> p (g v t)"),
                                      halfword(K[i])).then_inc(db.step(f"kt{i}"), 1)
                if ph == "bq3":
                    for i in (1, 3):
                        dve.wait_ge(*pb.at(f"qt{i}", b))
                        v.tensor_copy(q_t[:, 4 * i:4 * i + 4, :].rearrange("p h t -> p (h t)"), halfword(K[i]))\
                            .then_inc(db.step(f"qt{i}"), 1)
                if ph == "bq2":
                    qr = xq[:, :, :].rearrange("p t (h d) -> p (t h) d", d=HD1)
                    xf = x4[:, :, :].rearrange("p t (h d) -> p (t h) d", d=HD1)
                    dve.wait_ge(*ab.at("qh", b))
                    v.tensor_tensor(qr, xf, q_sl[:, :, 0:8], ALU.subtract).then_inc(db.step("qr"), 1)
                    v.tensor_copy(q_sl[:, :, 8:16], q_sl[:, :, 0:8]).then_inc(db.step(), 1)
                    v.tensor_copy(q_sl[:, :, 32:40], q_sl[:, :, 0:8]).then_inc(db.step(), 1)
                    dve.wait_ge(*ab.at("qm", b))
                    v.tensor_tensor(qr, qr, q_sl[:, :, 16:24], ALU.subtract).then_inc(db.step("qr2"), 1)
                    v.tensor_copy(q_sl[:, :, 24:32], q_sl[:, :, 16:24]).then_inc(db.step("qsl"), 1)
                if ph in BMAX:
                    for c in range(2):
                        n = 2 * BMAX.index(ph) + c
                        s, hp = divmod(n, HQ // 2)
                        dve.wait_ge(*pb.at(f"ms{n}", b))
                        v.tensor_reduce(nmx[:, s, 2 * hp:2 * hp + 2], two(K[n % 4]), AX_X, ALU.max, negate=True)\
                            .then_inc(db.step(f"mx{n}"), 1)
                    if ph == BMAX[-1]:
                        own(db, b)
                        v.tensor_copy(nmb[:, :, :], nmx[:, :, :]).then_inc(db.step("nmb"), 1)
                if ph in BG or ph == "ba1":
                    g = BG.index(ph) // 2 - 1 if ph in BG else HKV - 1
                    if g >= 0 and (ph == "ba1" or ph.endswith("a")):
                        dve.wait_ge(*pb.at(f"av{g}", b))
                        v.tensor_copy(ao[:, g, :], K[2 + g % 2][:, 0:S]).then_inc(db.step(f"ao{g}"), 1)
                if ph == "ba2":
                    for i in range(4):
                        s, half = divmod(i, 2)
                        dve.wait_ge(*pb.at(f"ot{i}", b))
                        o = K[i][:, :].rearrange("p (h c) -> p h c", c=32)
                        v.reciprocal(rec[:, i, :], o[:, :, HD1:HD1 + 1].rearrange("p h o -> p (h o)"))\
                            .then_inc(db.step(), 1)
                        own(db, b)
                        v.tensor_tensor(xq[:, s, half * P:half * P + P].rearrange("p (h d) -> p h d", d=HD1),
                                        o[:, :, 0:HD1], rec[:, i, :].unsqueeze(2).to_broadcast([P, 16, HD1]),
                                        ALU.mult).then_inc(db.step(), 1)
                    own(db, b)
                    v.tensor_tensor(xqf, xqf, x4f, ALU.add).then_inc(db.step("x4_read"), 1)
                    if later(b):
                        dve.wait_ge(out_done, b * 16)
                    layernorm(b, xq, x5, db, gb, "ln5", st6b, mvb, veb, rsb)
                    db.number["x5"] = db.count
                if ph == "br2":
                    dve.wait_ge(*ab.at("lg1", b))
                    v.tensor_reduce(smb[:, 0:2], lg1[:, :, 0:E1], AX_X, ALU.max, negate=True)\
                        .then_inc(db.step("nm1"), 1)
                    dve.wait_ge(*ab.at("tsg", b))
                    v.reciprocal(smb[:, 6:8], smb[:, 2:4]).then_inc(db.step(), 1)
                    v.tensor_scalar(cb[:, :, E1:E1 + 1], smb[:, 4:6].unsqueeze(2), 0.5, 0.5, ALU.mult, ALU.add)\
                        .then_inc(db.step(), 1)
                    own(db, b)
                    for t in range(TT):
                        v.tensor_scalar(pr1[:, t, 0:E1], pr1[:, t, 0:E1], smb[:, 6 + t:7 + t], None, ALU.mult)\
                            .then_inc(db.step(), 1)
                    own(db, b)
                    top(pr1, v81, tr1, rp1, TOP1, E1, db, b)
                    v.scalar_tensor_tensor(cb[:, :, 0:E1], rp1[:, :, 0:E1], 2 * NEG, pr1[:, :, 0:E1], ALU.is_equal,
                                           ALU.mult).then_inc(db.step(), 1)
                    own(db, b)
                    v.tensor_reduce(smb[:, 8:10], cb[:, :, 0:E1], AX_X, ALU.add).then_inc(db.step(), 1)
                    own(db, b)
                    v.tensor_scalar(smb[:, 10:12], smb[:, 8:10], 1e-9, None, ALU.max).then_inc(db.step(), 1)
                    own(db, b)
                    v.reciprocal(smb[:, 12:14], smb[:, 10:12]).then_inc(db.step(), 1)
                    own(db, b)
                    for t in range(TT):
                        v.tensor_scalar(cb[:, t, 0:E1], cb[:, t, 0:E1], smb[:, 12 + t:13 + t], None, ALU.mult)\
                            .then_inc(db.step(), 1)
                    src = cb
                    for k in range(3):
                        own(db, b)
                        part = cp[:, :, 32 * k:32 * k + 32]
                        v.tensor_copy(part, src[:, :, :]).then_inc(db.step("cp"), 1)
                        if k < 2:
                            own(db, b)
                            v.tensor_tensor(cbr[:, :, :], src[:, :, :], part, ALU.subtract).then_inc(db.step(), 1)
                            src = cbr
                if ph in BE:
                    m = BE.index(ph)
                    dve.wait_ge(*ab.at(f"th{m}", b))
                    v.scalar_tensor_tensor(thg[:, m % 2, :], thg[:, m % 2, :], 1.0, K[m % 2][:, 0:S], ALU.add,
                                           ALU.mult).then_inc(db.step(), 1)
                    if m >= 2:
                        dve.wait_ge(*gb.at(f"hid{m - 2}", b))
                    own(db, b)
                    v.tensor_tensor(hraw[:, m % 2, :], thg[:, m % 2, :], K[m % 2][:, S:2 * S], ALU.mult)\
                        .then_inc(db.step(f"gu{m}"), 1)
                if ph == "bout":
                    dve.wait_ge(*pb.at(f"down{MT1 - 1}", b))
                    v.tensor_tensor(xqf, K[3][:, :], x5f, ALU.add).then_inc(db.step(), 1)
                    layernorm(b, xq, x5, db, gb, "ln6", st6b, mvb, veb, rsb)
                    db.number["y"] = db.count

            run(dve, front, back, [df], [db], ORDER_DVE)

    return {n: {"total": s.seen, "number": s.number} for n, s in steps.items()}


def kernel(**inputs):
    import numpy as np
    import concourse.bacc as bacc
    from concourse.bass_utils import run_bass_kernel_spmd

    i = {k: np.ascontiguousarray(v) for k, v in inputs.items()}
    f = np.float32

    def tiles(w, rows_=None):
        k, n = w.shape
        t = -(-k // P)
        full = np.zeros((t * P, n), f)
        full[:k] = w
        return full.reshape(t, P, n).transpose(1, 0, 2)

    def wide(w, n):
        full = np.zeros((w.shape[0], n), f)
        full[:, :w.shape[1]] = w
        return full

    def flat(*parts):
        return np.ascontiguousarray(np.concatenate([p.reshape(p.shape[0], -1) for p in parts], axis=1))

    def lora_a(experts, shared):
        return np.concatenate([experts.transpose(1, 0, 2).reshape(shared.shape[0], -1), shared], axis=1)

    def lora_b(experts, shared):
        return np.concatenate([experts.reshape(-1, shared.shape[1]), shared], axis=0)

    p = np.arange(P)[:, None]
    m = np.arange(S)[None, :]
    consts = np.concatenate([
        np.eye(P, dtype=f), np.maximum(m - p, 0).astype(f), (m >= p).astype(f),
        (p // HD0 == np.arange(8)[None, :]).astype(f), (p % 32 == np.arange(32)[None, :]).astype(f)], axis=1)
    bcs = np.where(p < NS, 0.25, 0.5).astype(f)

    def column(v):
        return v.reshape(-1, P).T

    bk_col = np.zeros((P, 1), f)
    bk_col[:CD, 0] = i["L0_xattn_b_k"]
    cw = i["L1_attn_conv_w"].reshape(NCONV, DT, P).transpose(2, 1, 0)
    al = i["L1_attn_A_log"].reshape(DT, P, NS).transpose(1, 0, 2)
    arrays = {
        "consts": consts,
        "vec": flat(column(i["L1_attn_w_norm"]), cw, column(i["L1_attn_conv_b"]), column(i["L1_attn_b_dt"]),
                    column(i["L1_attn_D"]), al, bk_col, bcs),
        "rows": np.ascontiguousarray(np.broadcast_to(np.concatenate([
            i["L0_xattn_ln_gamma"], i["L0_xattn_ln_beta"], i["L0_xattn_b_k"], i["L0_ffn_expert_bias"],
            i["L0_attn_slope_rate"].reshape(-1)])[None, :], (P, R_END))),
        "w_l0": flat(tiles(i["L0_attn_W_qkvu"].T), tiles(i["L0_attn_W_out"].T)),
        "wk": np.ascontiguousarray(i["L0_xattn_W_k"].T),
        "w_f": flat(tiles(wide(i["L0_ffn_W_gate"], MT0 * P)), tiles(wide(i["L0_ffn_W_up"], MT0 * P)),
                    tiles(np.concatenate([i["L0_ffn_W_down"], lora_a(i["L0_ffn_A_down"], i["L0_ffn_sA_down"])], 1)),
                    tiles(np.concatenate([i["L0_ffn_W_router"], lora_a(i["L0_ffn_A_gate"], i["L0_ffn_sA_gate"]),
                                          lora_a(i["L0_ffn_A_up"], i["L0_ffn_sA_up"])], 1))),
        "w_lb": flat(wide(lora_b(i["L0_ffn_B_gate"], i["L0_ffn_sB_gate"]), MT0 * P),
                     wide(lora_b(i["L0_ffn_B_up"], i["L0_ffn_sB_up"]), MT0 * P),
                     lora_b(i["L0_ffn_B_down"], i["L0_ffn_sB_down"])),
        "w_m": flat(tiles(i["L1_attn_W_in"]), tiles(i["L1_attn_W_xp"]), i["L1_attn_W_dt"],
                    tiles(i["L1_attn_W_out"])),
        "wr1": tiles(np.concatenate([i["L1_ffn_router_w"].T, i["L1_ffn_sh_gate_w"]], 1)),
    }

    def units(experts, shared):
        w = np.zeros((D, MT1 * P), f)
        w[:, :E1 * IE] = experts.transpose(1, 0, 2).reshape(D, -1)
        w[:, E1 * IE:E1 * IE + ISH] = shared
        return w.reshape(KT, P, MT1, P).transpose(2, 1, 0, 3).reshape(MT1, P, -1)

    down = np.zeros((MT1 * P, D), f)
    down[:E1 * IE] = i["L1_ffn_w_down"].reshape(-1, D)
    down[E1 * IE:E1 * IE + ISH] = i["L1_ffn_sh_down"]
    arrays["w_moe"] = np.concatenate([units(i["L1_ffn_w_gate"], i["L1_ffn_sh_gate"]),
                                      units(i["L1_ffn_w_up"], i["L1_ffn_sh_up"]), down.reshape(MT1, P, D)], axis=2)
    x, c = i["x"], i["ctx_512"]
    arrays["x_tok"] = x.reshape(B, TT, P, D).transpose(0, 2, 1, 3)
    arrays["x_t"] = x.transpose(0, 2, 1).reshape(B, KT, P, S).transpose(0, 2, 1, 3)
    arrays["c_tok"] = c.reshape(B, TT, P, CD).transpose(0, 2, 1, 3)
    arrays["ctx_t"] = c.transpose(0, 2, 1)
    arrays = {k: np.ascontiguousarray(v) for k, v in arrays.items()}

    def program(known):
        nc = bacc.Bacc("TRN2", target_bir_lowering=False, num_devices=1)
        ins = {k: nc.dram_tensor("in_" + k, v.shape, mybir.dt.from_np(v.dtype), kind="ExternalInput").ap()
               for k, v in arrays.items()}
        out = nc.dram_tensor("y", (B, S, D), F32, kind="ExternalOutput").ap()
        return nc, build(nc, ins, out, known)

    _, known = program({})
    nc, _ = program(known)
    r = run_bass_kernel_spmd(nc, [{"in_" + k: v for k, v in arrays.items()}], core_ids=[0])
    return r.results[0]["y"]
```
